# Optimizing a Trainium2 kernel written in Bass

```python
import numpy as np
import jax
import jax.numpy as jnp

def _softmax(x, axis=-1):
    return jax.nn.softmax(x, axis=axis)

def _gelu(x):
    return jax.nn.gelu(x, approximate=True)

def _silu(x):
    return jax.nn.silu(x)

def _sigmoid(x):
    return jax.nn.sigmoid(x)

def _layernorm(x, axis=-1, eps=1e-05):
    m = jnp.mean(x, axis=axis, keepdims=True)
    v = jnp.var(x, axis=axis, keepdims=True)
    return (x - m) / jnp.sqrt(v + eps)

def _scatter_add(tgt, idx, src, axis=0):
    return tgt.at[idx].add(src)

def _segment_sum(src, seg, n):
    return jax.ops.segment_sum(src, seg, n)
kernel_name = 'mk_adj_preln_d2_adj_r2_0f3a91'

def setup_inputs(seed: int=0):
    np.random.seed(seed)
    _w = jnp.asarray

    def _rec_inputs():
        import jax
        import jax.numpy as jnp
        _gk = jax.random.key(seed)
        x = -0.0005207 + 1.001 * jax.random.normal(jax.random.fold_in(_gk, 1), (8, 1024, 128), jnp.float32)
        _a = jax.random.bernoulli(jax.random.fold_in(_gk, 2), 0.015625, (8, 1024, 1024))
        _af = _a.astype(jnp.float32)
        adj = _af
        return (x, adj)
    x, adj = _rec_inputs()

    def _L0_gnn_setup():
        import jax, jax.numpy as jnp
        import numpy as np
        import math
        B, N, F_IN, F_OUT = (8, 1024, 128, 128)

        def _uniform(key, shape, stdv):
            return jax.random.uniform(key, shape, dtype=jnp.float32, minval=-stdv, maxval=stdv)
        key = jax.random.key(seed)
        k_x, k_a, k_w, k_att, k_bw, k_ba = jax.random.split(key, 6)
        X = jax.random.normal(k_x, (B, N, F_IN), dtype=jnp.float32)
        A = jax.random.randint(k_a, (B, N, N), 0, 2).astype(jnp.float32)
        stdv_W = 1.0 / math.sqrt(F_OUT)
        stdv_a = 1.0 / math.sqrt(2 * F_OUT)
        W = _uniform(k_w, (F_IN, F_OUT), stdv_W)
        a = _uniform(k_att, (1, 2 * F_OUT), stdv_a)
        bias_W = _uniform(k_bw, (F_OUT,), stdv_W)
        bias_a = _uniform(k_ba, (N,), stdv_a)
        return {'X': X, 'A': A, 'W': W, 'a': a, 'bias_a': bias_a, 'bias_W': bias_W}
    _L0_gnn_all = _L0_gnn_setup()
    _L0_gnn_in = {k: v for k, v in _L0_gnn_all.items() if k in ('W', 'a', 'bias_a', 'bias_W')}
    del _L0_gnn_all

    def _L1_gnn_setup():
        import jax, jax.numpy as jnp
        import numpy as np
        key = jax.random.key(seed)
        k1, k2, k3, k4 = jax.random.split(key, 4)
        B, N, Fin, Fout = (16, 1024, 128, 128)
        clip = jax.random.normal(k1, (B, N, Fin), dtype=jnp.float32)
        adj_mat = jax.random.uniform(k2, (B, N, N), dtype=jnp.float32)
        limit = float(np.sqrt(6.0 / (Fin + Fout)))
        W = jax.random.uniform(k3, (Fout, Fin), minval=-limit, maxval=limit, dtype=jnp.float32)
        bias = jnp.zeros((Fout,), dtype=jnp.float32)
        prelu_a = jax.random.uniform(k4, (1,), dtype=jnp.float32)
        return {'clip': clip, 'adj_mat': adj_mat, 'W': W, 'bias': bias, 'prelu_a': prelu_a}
    _L1_gnn_all = _L1_gnn_setup()
    _L1_gnn_in = {k: v for k, v in _L1_gnn_all.items() if k in ('W', 'bias', 'prelu_a')}
    del _L1_gnn_all
    return {'x': x, 'adj': adj, 'L0_gnn_W': _L0_gnn_in['W'], 'L0_gnn_a': _L0_gnn_in['a'], 'L0_gnn_bias_a': _L0_gnn_in['bias_a'], 'L0_gnn_bias_W': _L0_gnn_in['bias_W'], 'L1_gnn_W': _L1_gnn_in['W'], 'L1_gnn_bias': _L1_gnn_in['bias'], 'L1_gnn_prelu_a': _L1_gnn_in['prelu_a']}

def reference(x, adj, L0_gnn_W, L0_gnn_a, L0_gnn_bias_a, L0_gnn_bias_W, L1_gnn_W, L1_gnn_bias, L1_gnn_prelu_a):
    import jax
    import jax.numpy as jnp

    def _L0_gnn_ref(X, A, W, a, bias_a, bias_W):
        import jax, jax.numpy as jnp
        import numpy as np
        import math
        B, N, F_IN, F_OUT = (8, 1024, 128, 128)

        def _uniform(key, shape, stdv):
            return jax.random.uniform(key, shape, dtype=jnp.float32, minval=-stdv, maxval=stdv)
        XW = jnp.einsum('bnf,fo->bno', X, W)
        f = W.shape[1]
        a_j = a[0, :f]
        a_i = a[0, f:]
        s_j = jnp.einsum('bnf,f->bn', XW, a_j)
        s_i = jnp.einsum('bnf,f->bn', XW, a_i)
        Z1 = s_i[:, :, None] + s_j[:, None, :] + bias_a[None, None, :]
        den = jnp.exp(Z1)
        num = jnp.einsum('bik,bkj->bij', A, den)
        nz = num != 0
        att = jnp.where(nz, den / jnp.where(nz, num, 1.0), 0.0)
        buf = jnp.einsum('bij,bjf->bif', att, XW)
        H = jnp.einsum('bij,bjf->bif', A, buf) + bias_W
        return H

    def _L1_gnn_ref(clip, adj_mat, W, bias, prelu_a):
        import jax, jax.numpy as jnp
        import numpy as np
        clip_fc = jnp.einsum('bnf,of->bno', clip, W)
        graph_o = jnp.einsum('bnm,bmo->bno', adj_mat, clip_fc)
        graph_o = graph_o + bias
        return jnp.where(graph_o >= 0, graph_o, prelu_a[0] * graph_o)
    h = jnp.maximum(_layernorm(x, axis=-1), 0.0)
    x = x + _L0_gnn_ref(h, adj, L0_gnn_W, L0_gnn_a, L0_gnn_bias_a, L0_gnn_bias_W)
    h = jnp.maximum(_layernorm(x, axis=-1), 0.0)
    x = x + _L1_gnn_ref(h, adj, L1_gnn_W, L1_gnn_bias, L1_gnn_prelu_a)
    return x

_drawn_inputs = setup_inputs


def setup_inputs(seed=0):
    import zlib

    import numpy as np

    out = dict(_drawn_inputs(seed))
    spreads = {'L1_gnn_bias': (0.0, 2.0)}
    factors = {'L0_gnn_bias_a': 200.0, 'L0_gnn_bias_W': 200.0}
    for name, (base, spread) in spreads.items():
        noise = np.random.default_rng([zlib.crc32(name.encode()), seed]).standard_normal(out[name].shape)
        drawn = base * np.exp(spread * noise) if base else spread * noise
        out[name] = jnp.asarray(drawn.astype(out[name].dtype))
    for name, factor in factors.items():
        out[name] = (out[name] * factor).astype(out[name].dtype)
    return out
```

```python
from contextlib import ExitStack

import concourse.bass as bass
from concourse import mybir

F32 = mybir.dt.float32
BF16 = mybir.dt.bfloat16
F16 = mybir.dt.float16
ALU = mybir.AluOpType
ACT = mybir.ActivationFunctionType
AX_X = mybir.AxisListType.X

P = 128
SLOTS = 3
CHUNKS = 4
PARTS = 3
H_SCALE = 4096.0
EPS = 1e-5

CONSTS = 16 * 8
START = 1
FRONT, DOTS, ESPLIT, GSPLIT = 5, 2, 7, 8


class Batch:

    def __init__(self, k, d):
        self.index = SLOTS * k + d
        self.slot = d % SLOTS
        self.use = k + d // SLOTS
        self.k, self.d = k, d

    def count(self, per, n=0):
        value = (per * SLOTS) * self.k + (per * self.d + n + START)
        return max(value, START) if isinstance(value, int) else value


def build(nc, x, adj, w0, w0t, a, bias_a, bias_w, w1t, bias1, alpha, out):
    B, N, F = x.shape
    T = N // P
    HT = T // 2
    UC = T // CHUNKS
    assert B == 8 and F == P and HT * F == 512

    x_d = x.rearrange("b (p t) f -> b p (t f)", t=T)
    out_d = out.rearrange("b (p t) f -> b p (t f)", t=T)

    with ExitStack() as ctx:
        def sb(name, shape, dt=F32):
            return ctx.enter_context(nc.sbuf_tensor(name, shape, dt))

        def ring(name, shape, dt=F32):
            return [sb(f"{name}{s}", shape, dt) for s in range(SLOTS)]

        def psum(name, shape):
            return ctx.enter_context(nc.psum_tensor(name, shape, F32))

        def sem(name):
            return ctx.enter_context(nc.semaphore(name))

        raisers = {"dve": [], "pool": [], "act": [], "pe": []}

        def counted(name, by):
            raisers[by].append(sem(name))
            return raisers[by][-1]

        def start_counts(eng, by):
            for each in raisers[by]:
                eng.sem_inc(each, START)

        adj_sb = ring("adj_sb", [P, T, T, P])
        adj_hi = [s[:].rearrange("p u t q -> p (u t q)").bitcast(BF16)
                  .rearrange("p (u t q h) -> p u t q h", u=T, t=T, h=2)[:, :, :, :, 1] for s in adj_sb]
        x_sb = ring("x_sb", [P, T, F])
        xb_sb = ring("xb_sb", [P, T, F])
        r1_sb = ring("r1_sb", [P, T, F])
        x1_sb = ring("x1_sb", [P, T, F])
        hi_sb = ring("hi_sb", [P, T, F], F16)
        lo_sb = ring("lo_sb", [P, T, F], F16)
        out_sb = ring("out_sb", [P, T, F])
        e3_sb = ring("e3_sb", [P, T, PARTS], BF16)
        g3_sb = ring("g3_sb", [P, T, PARTS], BF16)
        ei_sb = ring("ei_sb", [P, 2 * T])
        w_sb = ring("w_sb", [P, T])
        nm1_sb = ring("nm1_sb", [P, T])
        nm2_sb = ring("nm2_sb", [P, T])
        v1_sb = ring("v1_sb", [P, T])
        v2_sb = ring("v2_sb", [P, T])
        rs1_sb = ring("rs1_sb", [P, T])
        rs2_sb = ring("rs2_sb", [P, T])
        nb2_sb = ring("nb2_sb", [P, T])

        h2_sb = sb("h2_sb", [P, T, F])
        gt_sb = sb("gt_sb", [P, T * P])
        pos_sb = sb("pos_sb", [P, T, F])
        neg_sb = sb("neg_sb", [P, T, F])
        px_sb = sb("px_sb", [P, T, F])
        hsb_sb = sb("hsb_sb", [P, P])
        prod_sb = sb("prod_sb", [P, 2 * T, F])
        dots_sb = sb("dots_sb", [P, 2, T])
        s_sb = sb("s_sb", [P, 2, T])
        st1_sb = sb("st1_sb", [P, T, 6])
        st2_sb = sb("st2_sb", [P, T, 6])
        sm_sb = sb("sm_sb", [P, 2, T, 2])
        df_sb = sb("df_sb", [P, 2, T])
        d2_sb = sb("d2_sb", [P, 2, T])
        vv_sb = sb("vv_sb", [P, 2, T])
        et_sb = sb("et_sb", [P, 4, T])
        gv_sb = sb("gv_sb", [P, 8, T])
        q_sb = sb("q_sb", [P, T])

        w0_sb = sb("w0_sb", [P, F])
        w0t_sb = sb("w0t_sb", [P, F])
        w1t_sb = sb("w1t_sb", [P, F])
        a_sb = sb("a_sb", [P, 2])
        ab_sb = sb("ab_sb", [P, 2, P])
        wa_sb = sb("wa_sb", [P, 2, F])
        ba_sb = sb("ba_sb", [P, T])
        bw_sb = sb("bw_sb", [P, F])
        b1_sb = sb("b1_sb", [P, F])
        b1r_sb = sb("b1r_sb", [P, 2, F])
        b1p_sb = sb("b1p_sb", [P, HT, F], BF16)
        b1h_sb = sb("b1h_sb", [P, 2, F], BF16)
        ones_sb = sb("ones_sb", [P, P], BF16)
        al_sb = sb("al_sb", [P, 1])
        nal_sb = sb("nal_sb", [P, 1])
        half_sb = sb("half_sb", [P, T])

        GT = psum("GT", [P, 2, 512])
        Y = psum("Y", [P, 2, 512])
        HS = psum("HS", [P, 512])
        S = psum("S", [P, 512])
        R = psum("R", [P, 512])
        Q = psum("Q", [P, 512])

        const_in = sem("const_in")
        x_in = [sem(f"x_in{s}") for s in range(SLOTS)]
        adj_in = [[sem(f"adj_in{s}_{c}") for c in range(CHUNKS)] for s in range(SLOTS)]
        out_stored = [counted(f"out_stored{s}", "act") for s in range(SLOTS)]
        ab_ready = sem("ab_ready")
        wa_done = sem("wa_done")
        wa_ready = sem("wa_ready")
        setup = sem("setup")
        half_ready = sem("half_ready")
        front_step = counted("front_step", "dve")
        nm1_ready = counted("nm1_ready", "dve")
        v1_ready = counted("v1_ready", "dve")
        dots_step = counted("dots_step", "dve")
        s_ready = counted("s_ready", "dve")
        e_step = counted("e_step", "dve")
        e_ready = counted("e_ready", "dve")
        w_ready = counted("w_ready", "dve")
        r_read = counted("r_read", "dve")
        g_step = counted("g_step", "dve")
        g_ready = counted("g_ready", "dve")
        q_read = counted("q_read", "dve")
        x1_ready = counted("x1_ready", "dve")
        back_step = counted("back_step", "dve")
        nm2_ready = counted("nm2_ready", "dve")
        v2_ready = counted("v2_ready", "dve")
        lo_ready = counted("lo_ready", "dve")
        out_ready = counted("out_ready", "dve")
        xb_ready = counted("xb_ready", "pool")
        rs1_ready = counted("rs1_ready", "pool")
        rs2_ready = counted("rs2_ready", "pool")
        nb2_ready = counted("nb2_ready", "pool")
        px_ready = counted("px_ready", "pool")
        r1_ready = counted("r1_ready", "act")
        exp_ready = counted("exp_ready", "act")
        h2_ready = counted("h2_ready", "act")
        hi_ready = counted("hi_ready", "act")
        gt_ready = counted("gt_ready", "act")
        pn_ready = counted("pn_ready", "act")
        hsb_ready = counted("hsb_ready", "act")
        r_done = counted("r_done", "pe")
        hs_done = counted("hs_done", "pe")
        s_done = counted("s_done", "pe")
        q_done = counted("q_done", "pe")
        gt_done = counted("gt_done", "pe")
        y_done = counted("y_done", "pe")

        def looped(eng, step):
            with eng.Fori(0, (B - 2) // SLOTS) as k:
                for j in range(SLOTS):
                    step(k, j)

        block = ctx.enter_context(nc.Block())

        @block.sync
        def _(sp):
            def load(t, into_used=True):
                if into_used:
                    sp.wait_ge(r1_ready, t.count(1, 1 - SLOTS))
                    sp.wait_ge(xb_ready, t.count(1, 1 - SLOTS))
                sp.dma_start(x_sb[t.slot][:].rearrange("p t f -> p (t f)"), x_d[t.index]).then_inc(x_in[t.slot], 16)
                if into_used:
                    sp.wait_ge(gt_done, t.count(2, 2 - 2 * SLOTS))
                for c in range(CHUNKS):
                    sp.dma_start(adj_sb[t.slot][:, UC * c:UC * (c + 1), :, :].rearrange("p u t q -> p (u t q)"),
                                 adj[t.index, :, UC * c:UC * (c + 1), :, :].rearrange("p u t q -> p (u t q)")
                                 ).then_inc(adj_in[t.slot][c], 16)

            load(Batch(0, 0), into_used=False)
            load(Batch(0, 1), into_used=False)
            looped(sp, lambda k, j: load(Batch(k, j + 2)))

        @block.gpsimd
        def _(pool):
            start_counts(pool, "pool")
            nc.gpsimd.memset(half_sb[:], -0.5).then_inc(half_ready, 1)
            pool.wait_ge(half_ready, 1)

            def add_bias(t):
                pool.wait_ge(x_in[t.slot], 16 * t.use + 16)
                pool.wait_ge(x1_ready, t.count(1, 1 - SLOTS))
                nc.gpsimd.tensor_tensor(xb_sb[t.slot][:], x_sb[t.slot][:],
                                        bw_sb[:].unsqueeze(1).broadcast_to((P, T, F)), ALU.add).then_inc(xb_ready, 1)

            def rstd1(t):
                pool.wait_ge(v1_ready, t.count(1, 1))
                pool.wait_ge(w_ready, t.count(1, 1 - SLOTS))
                nc.gpsimd.tensor_tensor(rs1_sb[t.slot][:], v1_sb[t.slot][:], half_sb[:], ALU.pow).then_inc(rs1_ready, 1)

            def rstd2(t):
                pool.wait_ge(v2_ready, t.count(1, 1))
                nc.gpsimd.tensor_tensor(rs2_sb[t.slot][:], v2_sb[t.slot][:], half_sb[:], ALU.pow).then_inc(rs2_ready, 1)
                pool.wait_ge(rs2_ready, t.count(1, 1))
                nc.gpsimd.tensor_tensor(nb2_sb[t.slot][:], nm2_sb[t.slot][:], rs2_sb[t.slot][:], ALU.mult).then_inc(nb2_ready, 1)

            def add_residual(t):
                pool.wait_ge(pn_ready, t.count(2, 1))
                pool.wait_ge(out_ready, t.count(1))
                nc.gpsimd.tensor_tensor(px_sb[:], pos_sb[:], x1_sb[t.slot][:], ALU.add).then_inc(px_ready, 1)

            def step(k, j):
                rstd1(Batch(k, j + 2))
                add_bias(Batch(k, j + 2))
                rstd2(Batch(k, j + 1))
                add_residual(Batch(k, j))

            pool.wait_ge(const_in, CONSTS)
            rstd1(Batch(0, 0))
            add_bias(Batch(0, 0))
            rstd1(Batch(0, 1))
            add_bias(Batch(0, 1))
            rstd2(Batch(0, 0))
            looped(pool, step)
            rstd2(Batch(0, 7))
            add_residual(Batch(0, 6))
            add_residual(Batch(0, 7))

        @block.vector
        def _(dve):
            tt, ts, stt = nc.vector.tensor_tensor, nc.vector.tensor_scalar, nc.vector.scalar_tensor_tensor

            def set_up():
                n = [0]

                def then(ins):
                    n[0] += 1
                    ins.then_inc(setup, 1)

                def settle():
                    dve.wait_ge(setup, n[0])

                then(nc.vector.memset(ones_sb[:], 1.0))
                then(nc.vector.memset(b1p_sb[:], 0.0))
                dve.wait_ge(const_in, CONSTS)
                nc.vector.tensor_copy(ab_sb[:, 0, :], a_sb[:, 1:2].broadcast_to((P, P))).then_inc(ab_ready, 1)
                nc.vector.tensor_copy(ab_sb[:, 1, :], a_sb[:, 0:1].broadcast_to((P, P))).then_inc(ab_ready, 1)
                then(ts(nal_sb[:], al_sb[:], -1.0, None, ALU.mult))
                then(nc.vector.tensor_copy(b1h_sb[:, 0, :], b1_sb[:]))
                settle()
                then(tt(b1r_sb[:, 0, :], b1_sb[:], b1h_sb[:, 0, :], ALU.subtract))
                settle()
                then(nc.vector.tensor_copy(b1h_sb[:, 1, :], b1r_sb[:, 0, :]))
                settle()
                then(tt(b1r_sb[:, 1, :], b1r_sb[:, 0, :], b1h_sb[:, 1, :], ALU.subtract))
                settle()
                for q, part in ((0, b1h_sb[0:1, 0, :]), (32, b1h_sb[32:33, 1, :]), (64, b1r_sb[64:65, 1, :])):
                    then(nc.vector.tensor_copy(b1p_sb[q:q + 1, :, :], part.unsqueeze(1).broadcast_to((1, HT, F))))
                dve.wait_ge(wa_done, 1)
                nc.vector.tensor_copy(wa_sb[:].rearrange("p i f -> p (i f)"), S[:, 0:2 * F]).then_inc(wa_ready, 1)
                return n[0]

            def statistics(t, layer, src, st, nm, v, step_sem, per, nm_ready, v_ready, scale):
                sm, df, d2, vv = sm_sb[:, layer], df_sb[:, layer], d2_sb[:, layer], vv_sb[:, layer]
                for u in range(T):
                    ins = nc.vector.bn_stats(st[:, u, :], src[:, u, :])
                ins.then_inc(step_sem, 1)
                dve.wait_ge(step_sem, t.count(per, 1))
                tt(sm, st[:, :, 1:3], st[:, :, 4:6], ALU.add).then_inc(step_sem, 1)
                tt(df, st[:, :, 1], st[:, :, 4], ALU.subtract).then_inc(step_sem, 1)
                dve.wait_ge(step_sem, t.count(per, 2))
                ts(nm, sm[:, :, 0], -0.5, None, ALU.mult).then_inc(nm_ready, 1)
                dve.wait_ge(step_sem, t.count(per, 3))
                tt(d2, df, df, ALU.mult).then_inc(step_sem, 1)
                dve.wait_ge(step_sem, t.count(per, 4))
                stt(vv, d2, F / 4.0, sm[:, :, 1], ALU.mult, ALU.add).then_inc(step_sem, 1)
                dve.wait_ge(step_sem, t.count(per, 5))
                ts(v, vv, scale / F, EPS * scale, ALU.mult, ALU.add).then_inc(v_ready, 1)

            def front(t):
                dve.wait_ge(x_in[t.slot], 16 * t.use + 16)
                statistics(t, 0, x_sb[t.slot], st1_sb, nm1_sb[t.slot][:], v1_sb[t.slot][:],
                           front_step, FRONT, nm1_ready, v1_ready, 1.0)

            def dots(t):
                dve.wait_ge(r1_ready, t.count(1, 1))
                for i in range(2):
                    for u in range(T):
                        ins = stt(prod_sb[:, i * T + u, :], r1_sb[t.slot][:, u, :], 1.0, wa_sb[:, i, :],
                                  ALU.mult, ALU.mult, accum_out=dots_sb[:, i, u:u + 1])
                ins.then_inc(dots_step, 1)
                dve.wait_ge(rs1_ready, t.count(1, 1))
                dve.wait_ge(dots_step, t.count(DOTS, 1))
                tt(s_sb[:], dots_sb[:], rs1_sb[t.slot][:].unsqueeze(1).broadcast_to((P, 2, T)), ALU.mult).then_inc(dots_step, 1)
                dve.wait_ge(dots_step, t.count(DOTS, 2))
                tt(s_sb[:, 1, :], s_sb[:, 1, :], ba_sb[:], ALU.add).then_inc(s_ready, 1)

            def split(value, parts, rest, step_sem, at, ready):
                nc.vector.tensor_copy(parts[:, :, 0], value).then_inc(step_sem, 1)
                dve.wait_ge(step_sem, at(1))
                tt(rest[0], value, parts[:, :, 0], ALU.subtract).then_inc(step_sem, 1)
                dve.wait_ge(step_sem, at(2))
                nc.vector.tensor_copy(parts[:, :, 1], rest[0]).then_inc(step_sem, 1)
                dve.wait_ge(step_sem, at(3))
                tt(parts[:, :, 2], rest[0], parts[:, :, 1], ALU.subtract).then_inc(ready, 1)

            def e_parts(t):
                dve.wait_ge(exp_ready, t.count(1, 1))
                ei, ej = ei_sb[t.slot][:, 0:T], ei_sb[t.slot][:, T:2 * T]
                split(ei, e3_sb[t.slot], [et_sb[:, 0, :]], e_step, lambda n: t.count(ESPLIT, n), e_ready)
                zero, div, inv, c = et_sb[:, 1, :], et_sb[:, 2, :], et_sb[:, 3, :], et_sb[:, 1, :]
                ts(zero, ej, 0.0, None, ALU.is_equal).then_inc(e_step, 1)
                dve.wait_ge(e_step, t.count(ESPLIT, 4))
                tt(div, zero, ej, ALU.add).then_inc(e_step, 1)
                dve.wait_ge(e_step, t.count(ESPLIT, 5))
                nc.vector.reciprocal(inv, div).then_inc(e_step, 1)
                dve.wait_ge(e_step, t.count(ESPLIT, 6))
                tt(c, ej, inv, ALU.mult).then_inc(e_step, 1)
                dve.wait_ge(e_step, t.count(ESPLIT, 7))
                tt(w_sb[t.slot][:], c, rs1_sb[t.slot][:], ALU.mult).then_inc(w_ready, 1)

            def g_parts(t):
                dve.wait_ge(r_done, t.count(1, 1))
                r, zero, div, inv, keep, g, rest = (gv_sb[:, i, :] for i in range(7))
                nc.vector.tensor_reduce(r, R[:, 0:4 * T].rearrange("p (u c) -> p u c", c=4)[:, :, 0:PARTS],
                                        AX_X, ALU.add).then_inc(r_read, 1)
                dve.wait_ge(r_read, t.count(1, 1))
                ts(zero, r, 0.0, None, ALU.is_equal).then_inc(g_step, 1)
                dve.wait_ge(g_step, t.count(GSPLIT, 1))
                tt(div, r, zero, ALU.add).then_inc(g_step, 1)
                dve.wait_ge(g_step, t.count(GSPLIT, 2))
                nc.vector.reciprocal(inv, div).then_inc(g_step, 1)
                dve.wait_ge(g_step, t.count(GSPLIT, 3))
                stt(keep, zero, 0.0, inv, ALU.is_equal, ALU.mult).then_inc(g_step, 1)
                dve.wait_ge(g_step, t.count(GSPLIT, 4))
                tt(g, keep, ei_sb[t.slot][:, 0:T], ALU.mult).then_inc(g_step, 1)
                dve.wait_ge(g_step, t.count(GSPLIT, 5))
                split(g, g3_sb[t.slot], [rest], g_step, lambda n: t.count(GSPLIT, 5 + n), g_ready)

            def add_attention(t):
                dve.wait_ge(q_done, t.count(1, 1))
                nc.vector.tensor_reduce(q_sb[:], Q[:, 0:4 * T].rearrange("p (u c) -> p u c", c=4)[:, :, 0:PARTS],
                                        AX_X, ALU.add).then_inc(q_read, 1)
                dve.wait_ge(q_read, t.count(1, 1))
                dve.wait_ge(s_done, t.count(1, 1))
                dve.wait_ge(xb_ready, t.count(1, 1))
                for u in range(T):
                    ins = stt(x1_sb[t.slot][:, u, :], S[:, 0:F], q_sb[:, u:u + 1], xb_sb[t.slot][:, u, :],
                              ALU.mult, ALU.add)
                ins.then_inc(x1_ready, 1)

            def middle(t):
                dve.wait_ge(x1_ready, t.count(1, 1))
                statistics(t, 1, x1_sb[t.slot], st2_sb, nm2_sb[t.slot][:], v2_sb[t.slot][:],
                           back_step, FRONT, nm2_ready, v2_ready, H_SCALE ** -2)

            def lower_part(t):
                dve.wait_ge(hi_ready, t.count(1, 1))
                tt(lo_sb[t.slot][:], h2_sb[:], hi_sb[t.slot][:], ALU.subtract).then_inc(lo_ready, 1)

            def finish(t):
                dve.wait_ge(px_ready, t.count(1, 1))
                dve.wait_ge(pn_ready, t.count(2, 2))
                dve.wait_ge(out_stored[t.slot], 16 * t.use + START)
                stt(out_sb[t.slot][:], neg_sb[:], nal_sb[:], px_sb[:], ALU.mult, ALU.add).then_inc(out_ready, 1)

            def step(k, j):
                front(Batch(k, j + 2))
                add_attention(Batch(k, j + 1))
                middle(Batch(k, j + 1))
                dots(Batch(k, j + 2))
                e_parts(Batch(k, j + 2))
                lower_part(Batch(k, j + 1))
                g_parts(Batch(k, j + 2))
                finish(Batch(k, j))

            start_counts(dve, "dve")
            n_setup = set_up()
            dve.wait_ge(setup, n_setup)
            dve.wait_ge(wa_ready, 1)
            front(Batch(0, 0))
            front(Batch(0, 1))
            dots(Batch(0, 0))
            e_parts(Batch(0, 0))
            dots(Batch(0, 1))
            e_parts(Batch(0, 1))
            g_parts(Batch(0, 0))
            add_attention(Batch(0, 0))
            middle(Batch(0, 0))
            g_parts(Batch(0, 1))
            lower_part(Batch(0, 0))
            looped(dve, step)
            add_attention(Batch(0, 7))
            middle(Batch(0, 7))
            finish(Batch(0, 6))
            lower_part(Batch(0, 7))
            finish(Batch(0, 7))

        @block.scalar
        def _(act):
            def relu_centred(t):
                act.wait_ge(x_in[t.slot], 16 * t.use + 16)
                act.wait_ge(nm1_ready, t.count(1, 1))
                act.wait_ge(hs_done, t.count(1, 1 - SLOTS))
                for u in range(T):
                    ins = nc.scalar.activation(r1_sb[t.slot][:, u, :], x_sb[t.slot][:, u, :], ACT.Relu,
                                               bias=nm1_sb[t.slot][:, u:u + 1])
                ins.then_inc(r1_ready, 1)

            def exponentials(t):
                act.wait_ge(s_ready, t.count(1, 1))
                nc.scalar.activation(ei_sb[t.slot][:], s_sb[:].rearrange("p i t -> p (i t)"), ACT.Exp).then_inc(exp_ready, 1)

            def normalise(t):
                act.wait_ge(nb2_ready, t.count(1, 1))
                act.wait_ge(lo_ready, t.count(1))
                for u in range(T):
                    ins = nc.scalar.activation(h2_sb[:, u, :], x1_sb[t.slot][:, u, :], ACT.Relu,
                                               scale=rs2_sb[t.slot][:, u:u + 1], bias=nb2_sb[t.slot][:, u:u + 1])
                ins.then_inc(h2_ready, 1)
                act.wait_ge(h2_ready, t.count(1, 1))
                nc.scalar.activation(hi_sb[t.slot][:], h2_sb[:], ACT.Copy).then_inc(hi_ready, 1)

            def copy_product(t):
                act.wait_ge(y_done, t.count(2))
                for h in range(2):
                    act.wait_ge(gt_done, t.count(2, h + 1))
                    nc.scalar.activation(gt_sb[:, 512 * h:512 * (h + 1)], GT[:, h, :], ACT.Copy,
                                         scale=1.0 / H_SCALE).then_inc(gt_ready, 1)

            def both_signs(t):
                act.wait_ge(y_done, t.count(2, 2))
                act.wait_ge(out_ready, t.count(1))
                y = Y[:].rearrange("p h (u f) -> p (h u) f", f=F)
                nc.scalar.activation(pos_sb[:], y, ACT.Relu).then_inc(pn_ready, 1)
                nc.scalar.activation(neg_sb[:], y, ACT.Relu, scale=-1.0).then_inc(pn_ready, 1)

            def spread_sum(t):
                act.wait_ge(hs_done, t.count(1, 1))
                act.wait_ge(s_done, t.count(1))
                nc.scalar.activation(hsb_sb[:], HS[:, 0:1].broadcast_to((P, P)), ACT.Copy).then_inc(hsb_ready, 1)

            def store(t):
                act.wait_ge(out_ready, t.count(1, 1))
                act.dma_start(out_d[t.index], out_sb[t.slot][:].rearrange("p t f -> p (t f)")).then_inc(out_stored[t.slot], 16)

            def step(k, j):
                relu_centred(Batch(k, j + 2))
                exponentials(Batch(k, j + 2))
                normalise(Batch(k, j + 1))
                copy_product(Batch(k, j))
                both_signs(Batch(k, j))
                spread_sum(Batch(k, j + 2))
                store(Batch(k, j))

            start_counts(act, "act")
            loads = [(w0t_sb, w0t), (a_sb, a), (b1_sb, bias1.unsqueeze(0).broadcast_to((P, F))), (w0_sb, w0), (w1t_sb, w1t),
                     (ba_sb, bias_a.rearrange("(p t) -> p t", t=T)), (bw_sb, bias_w.unsqueeze(0).broadcast_to((P, F))),
                     (al_sb, alpha.unsqueeze(0).broadcast_to((P, 1)))]
            assert 16 * len(loads) == CONSTS
            for dst, src in loads:
                act.dma_start(dst[:], src).then_inc(const_in, 16)
            relu_centred(Batch(0, 0))
            relu_centred(Batch(0, 1))
            exponentials(Batch(0, 0))
            exponentials(Batch(0, 1))
            spread_sum(Batch(0, 0))
            normalise(Batch(0, 0))
            spread_sum(Batch(0, 1))
            looped(act, step)
            normalise(Batch(0, 7))
            for d in (6, 7):
                copy_product(Batch(0, d))
                both_signs(Batch(0, d))
                store(Batch(0, d))
            for s in range(SLOTS):
                act.wait_ge(out_stored[s], 16 * len(range(s, B, SLOTS)) + START)

        @block.tensor
        def _(pe):
            mm = nc.tensor.matmul

            def set_up():
                pe.wait_ge(const_in, CONSTS)
                for i in range(2):
                    pe.wait_ge(ab_ready, i + 1)
                    ins = mm(S[:, F * i:F * (i + 1)], ab_sb[:, i, :], w0t_sb[:], start=True, stop=True)
                ins.then_inc(wa_done, 1)

            def times_adj(bank, parts, t, done, chunks):
                for u in range(T):
                    if chunks and u % UC == 0:
                        pe.wait_ge(adj_in[t.slot][u // UC], 16 * t.use + 16)
                    for c in range(T):
                        ins = mm(bank[:, 4 * u:4 * u + PARTS], adj_hi[t.slot][:, u, c, :], parts[t.slot][:, c, :],
                                 start=(c == 0), stop=(c == T - 1))
                ins.then_inc(done, 1)

            def row_sums(t):
                pe.wait_ge(e_ready, t.count(1, 1))
                pe.wait_ge(r_read, t.count(1))
                times_adj(R, e3_sb, t, r_done, True)

            def column_sums(t):
                pe.wait_ge(w_ready, t.count(1, 1))
                for u in range(T):
                    ins = mm(HS[:, 0:1], r1_sb[t.slot][:, u, :], w_sb[t.slot][:, u:u + 1], start=(u == 0), stop=(u == T - 1))
                ins.then_inc(hs_done, 1)
                pe.wait_ge(hsb_ready, t.count(1, 1))
                pe.wait_ge(x1_ready, t.count(1))
                mm(S[:, 0:F], hsb_sb[:], w0_sb[:], start=True, stop=True).then_inc(s_done, 1)

            def weighted(t):
                pe.wait_ge(g_ready, t.count(1, 1))
                pe.wait_ge(q_read, t.count(1))
                times_adj(Q, g3_sb, t, q_done, False)

            def product(t):
                pe.wait_ge(lo_ready, t.count(1, 1))
                pe.wait_ge(gt_ready, t.count(2))
                for h in range(2):
                    for c in range(T):
                        for part in (hi_sb, lo_sb):
                            ins = mm(GT[:, h, :], part[t.slot][:, c, :], adj_hi[t.slot][:, HT * h:HT * (h + 1), c, :],
                                     start=(c == 0 and part is hi_sb), stop=(c == T - 1 and part is lo_sb))
                    ins.then_inc(gt_done, 1)

            def project(t):
                pe.wait_ge(pn_ready, t.count(2))
                for h in range(2):
                    mm(Y[:, h, :], ones_sb[:], b1p_sb[:].rearrange("p u f -> p (u f)"), start=True, stop=False)
                    pe.wait_ge(gt_ready, t.count(2, h + 1))
                    for u in range(HT):
                        at = HT * h + u
                        ins = mm(Y[:, h, F * u:F * (u + 1)], gt_sb[:, P * at:P * (at + 1)], w1t_sb[:],
                                 start=False, stop=(u == HT - 1))
                    ins.then_inc(y_done, 1)

            def step(k, j):
                row_sums(Batch(k, j + 1))
                column_sums(Batch(k, j + 1))
                weighted(Batch(k, j + 1))
                product(Batch(k, j))
                project(Batch(k, j))

            start_counts(pe, "pe")
            set_up()
            row_sums(Batch(0, 0))
            column_sums(Batch(0, 0))
            weighted(Batch(0, 0))
            looped(pe, step)
            row_sums(Batch(0, 7))
            column_sums(Batch(0, 7))
            weighted(Batch(0, 7))
            for d in (6, 7):
                product(Batch(0, d))
                project(Batch(0, d))


def kernel(x, adj, L0_gnn_W, L0_gnn_a, L0_gnn_bias_a, L0_gnn_bias_W, L1_gnn_W, L1_gnn_bias, L1_gnn_prelu_a):
    import numpy as np
    import concourse.bacc as bacc
    from concourse.bass_utils import run_bass_kernel_spmd

    B, N, F = x.shape
    T = N // P
    arrays = {
        "x": np.asarray(x),
        "adj": np.asarray(adj).reshape(B, P, T, P, T).transpose(0, 3, 2, 4, 1),
        "w0": np.asarray(L0_gnn_W),
        "w0t": np.asarray(L0_gnn_W).T,
        "a": np.asarray(L0_gnn_a).reshape(2, F).T,
        "bias_a": np.asarray(L0_gnn_bias_a),
        "bias_w": np.asarray(L0_gnn_bias_W),
        "w1t": np.asarray(L1_gnn_W).T,
        "bias1": np.asarray(L1_gnn_bias),
        "alpha": np.asarray(L1_gnn_prelu_a),
    }
    arrays = {name: np.ascontiguousarray(v) for name, v in arrays.items()}
    nc = bacc.Bacc("TRN2", target_bir_lowering=False, num_devices=1)
    args = [nc.dram_tensor(name, v.shape, mybir.dt.from_np(v.dtype), kind="ExternalInput").ap() for name, v in arrays.items()]
    args.append(nc.dram_tensor("out", (B, N, F), F32, kind="ExternalOutput").ap())
    build(nc, *args)
    result = run_bass_kernel_spmd(nc, [arrays], core_ids=[0])
    return result.results[0]["out"]
```

```python
from contextlib import ExitStack

import concourse.bass as bass
from concourse import mybir

F32 = mybir.dt.float32
BF16 = mybir.dt.bfloat16
F16 = mybir.dt.float16
ALU = mybir.AluOpType
ACT = mybir.ActivationFunctionType
AX_X = mybir.AxisListType.X

P = 128
SLOTS = 3
CHUNKS = 4
PARTS = 3
H_SCALE = 4096.0
EPS = 1e-5

CONSTS = 16 * 8
START = 1
FRONT, DOTS, ESPLIT, GSPLIT = 5, 3, 1, 5


class Batch:

    def __init__(self, k, d):
        self.index = SLOTS * k + d
        self.slot = d % SLOTS
        self.use = k + d // SLOTS
        self.k, self.d = k, d

    def count(self, per, n=0):
        value = (per * SLOTS) * self.k + (per * self.d + n + START)
        return max(value, START) if isinstance(value, int) else value


def build(nc, x, adj, w0, w0t, a, bias_a, bias_w, w1t, bias1, alpha, out):
    B, N, F = x.shape
    T = N // P
    HT = T // 2
    UC = T // CHUNKS
    assert B == 8 and F == P and HT * F == 512

    x_d = x.rearrange("b (p t) f -> b p (t f)", t=T)
    out_d = out.rearrange("b (p t) f -> b p (t f)", t=T)

    with ExitStack() as ctx:
        def sb(name, shape, dt=F32):
            return ctx.enter_context(nc.sbuf_tensor(name, shape, dt))

        def ring(name, shape, dt=F32):
            return [sb(f"{name}{s}", shape, dt) for s in range(SLOTS)]

        def psum(name, shape):
            return ctx.enter_context(nc.psum_tensor(name, shape, F32))

        def sem(name):
            return ctx.enter_context(nc.semaphore(name))

        raisers = {"dve": [], "pool": [], "act": [], "pe": []}

        def counted(name, by):
            raisers[by].append(sem(name))
            return raisers[by][-1]

        def start_counts(eng, by):
            for each in raisers[by]:
                eng.sem_inc(each, START)

        def upper(words, dims, **sizes):
            halves = words.rearrange(f"p {dims} -> p ({dims})").bitcast(BF16)
            return halves.rearrange(f"p ({dims} h) -> p {dims} h", h=2, **sizes)[(slice(None),) * (len(sizes) + 2) + (1,)]

        adj_sb = ring("adj_sb", [P, T, T, P])
        adj_hi = [upper(s[:], "u t q", u=T, t=T) for s in adj_sb]
        x_sb = ring("x_sb", [P, T, F])
        xb_sb = ring("xb_sb", [P, T, F])
        r1_sb = ring("r1_sb", [P, T, F])
        x1_sb = ring("x1_sb", [P, T, F])
        hi_sb = ring("hi_sb", [P, T, F], F16)
        lo_sb = ring("lo_sb", [P, T, F], F16)
        out_sb = ring("out_sb", [P, T, F])
        e3_sb = ring("e3_sb", [P, T, PARTS])
        g3_sb = ring("g3_sb", [P, T, PARTS])
        e3_hi = [upper(s[:], "t c", t=T) for s in e3_sb]
        g3_hi = [upper(s[:], "t c", t=T) for s in g3_sb]
        ej_sb = ring("ej_sb", [P, T])
        w_sb = ring("w_sb", [P, T])
        nm1_sb = ring("nm1_sb", [P, T])
        nm2_sb = ring("nm2_sb", [P, T])
        v1_sb = ring("v1_sb", [P, T])
        v2_sb = ring("v2_sb", [P, T])
        rs1_sb = ring("rs1_sb", [P, T])
        rs2_sb = ring("rs2_sb", [P, T])
        nb2_sb = ring("nb2_sb", [P, T])

        h2_sb = sb("h2_sb", [P, T, F])
        gt_sb = sb("gt_sb", [P, T * P])
        pos_sb = sb("pos_sb", [P, T, F])
        neg_sb = sb("neg_sb", [P, T, F])
        px_sb = sb("px_sb", [P, T, F])
        hr_sb = sb("hr_sb", [P, F])
        hsb_sb = sb("hsb_sb", [P, P])
        quarter_sb = sb("quarter_sb", [P, P])
        ssb_sb = sb("ssb_sb", [P, F])
        prod_sb = sb("prod_sb", [P, T, F])
        dots_sb = sb("dots_sb", [P, 2, T])
        s_sb = sb("s_sb", [P, 2, T])
        sj_sb = sb("sj_sb", [P, T])
        st1_sb = sb("st1_sb", [P, T, 6])
        st2_sb = sb("st2_sb", [P, T, 6])
        sm_sb = sb("sm_sb", [P, 2, T, 2])
        df_sb = sb("df_sb", [P, 2, T])
        d2_sb = sb("d2_sb", [P, 2, T])
        vv_sb = sb("vv_sb", [P, 2, T])
        gv_sb = sb("gv_sb", [P, 4, T])
        q_sb = sb("q_sb", [P, T])

        w0_sb = sb("w0_sb", [P, F])
        w0t_sb = sb("w0t_sb", [P, F])
        w1t_sb = sb("w1t_sb", [P, F])
        a_sb = sb("a_sb", [P, 2])
        ab_sb = sb("ab_sb", [P, 2, P])
        wa_sb = sb("wa_sb", [P, 2, F])
        ba_sb = sb("ba_sb", [P, T])
        bw_sb = sb("bw_sb", [P, F])
        b1_sb = sb("b1_sb", [P, F])
        b1r_sb = sb("b1r_sb", [P, 2, F])
        b1p_sb = sb("b1p_sb", [P, HT, F], BF16)
        b1h_sb = sb("b1h_sb", [P, 2, F], BF16)
        ones_sb = sb("ones_sb", [P, P], BF16)
        al_sb = sb("al_sb", [P, 1])
        nal_sb = sb("nal_sb", [P, 1])
        zero_sb = sb("zero_sb", [P, 1])
        warm_sb = sb("warm_sb", [P, 1])
        half_sb = sb("half_sb", [P, T])

        GT = psum("GT", [P, 2, 512])
        Y = psum("Y", [P, 2, 512])
        HS = psum("HS", [P, 512])
        S = psum("S", [P, 512])
        R = psum("R", [P, 512])
        Q = psum("Q", [P, 512])

        const_in = sem("const_in")
        x_in = [sem(f"x_in{s}") for s in range(SLOTS)]
        adj_in = [[sem(f"adj_in{s}_{c}") for c in range(CHUNKS)] for s in range(SLOTS)]
        out_stored = [counted(f"out_stored{s}", "act") for s in range(SLOTS)]
        ab_ready = sem("ab_ready")
        wa_done = sem("wa_done")
        wa_ready = sem("wa_ready")
        setup = sem("setup")
        half_ready = sem("half_ready")
        zero_ready = sem("zero_ready")
        warmed = sem("warmed")
        front_step = counted("front_step", "dve")
        nm1_ready = counted("nm1_ready", "dve")
        v1_ready = counted("v1_ready", "dve")
        dots_step = counted("dots_step", "dve")
        si_ready = counted("si_ready", "dve")
        sj_ready = counted("sj_ready", "dve")
        e_step = counted("e_step", "dve")
        e_ready = counted("e_ready", "dve")
        w_ready = counted("w_ready", "dve")
        r_read = counted("r_read", "dve")
        g_step = counted("g_step", "dve")
        g_ready = counted("g_ready", "dve")
        q_read = counted("q_read", "dve")
        x1_ready = counted("x1_ready", "dve")
        back_step = counted("back_step", "dve")
        nm2_ready = counted("nm2_ready", "dve")
        v2_ready = counted("v2_ready", "dve")
        out_ready = counted("out_ready", "dve")
        xb_ready = counted("xb_ready", "pool")
        rs1_ready = counted("rs1_ready", "pool")
        rs2_ready = counted("rs2_ready", "pool")
        nb2_ready = counted("nb2_ready", "pool")
        px_ready = counted("px_ready", "pool")
        lo_ready = counted("lo_ready", "pool")
        r1_ready = counted("r1_ready", "act")
        ei_ready = counted("ei_ready", "act")
        ej_ready = counted("ej_ready", "act")
        h2_ready = counted("h2_ready", "act")
        hi_ready = counted("hi_ready", "act")
        gt_ready = counted("gt_ready", "act")
        pn_ready = counted("pn_ready", "act")
        hr_ready = counted("hr_ready", "act")
        hsb_ready = counted("hsb_ready", "act")
        ssb_ready = counted("ssb_ready", "act")
        r_done = counted("r_done", "pe")
        hs_done = counted("hs_done", "pe")
        turned = counted("turned", "pe")
        s_done = counted("s_done", "pe")
        q_done = counted("q_done", "pe")
        gt_done = counted("gt_done", "pe")
        y_done = counted("y_done", "pe")

        def looped(eng, step):
            with eng.Fori(0, (B - 2) // SLOTS) as k:
                for j in range(SLOTS):
                    step(k, j)

        block = ctx.enter_context(nc.Block())

        @block.sync
        def _(sp):
            def load_x(t, into_used=True):
                if into_used:
                    sp.wait_ge(r1_ready, t.count(1, 1 - SLOTS))
                    sp.wait_ge(xb_ready, t.count(1, 1 - SLOTS))
                sp.dma_start(x_sb[t.slot][:].rearrange("p t f -> p (t f)"), x_d[t.index]).then_inc(x_in[t.slot], 16)

            def load_adj(t, into_used=True):
                if into_used:
                    sp.wait_ge(gt_done, t.count(2, 2 - 2 * SLOTS))
                for c in range(CHUNKS):
                    sp.dma_start(adj_sb[t.slot][:, UC * c:UC * (c + 1), :, :].rearrange("p u t q -> p (u t q)"),
                                 adj[t.index, :, UC * c:UC * (c + 1), :, :].rearrange("p u t q -> p (u t q)")
                                 ).then_inc(adj_in[t.slot][c], 16)

            def step(k, j):
                load_x(Batch(k, j + 2))
                load_adj(Batch(k, j + 2))

            load_x(Batch(0, 0), into_used=False)
            sp.dma_start(w0_sb[:], w0).then_inc(const_in, 16)
            sp.dma_start(bw_sb[:], bias_w.unsqueeze(0).broadcast_to((P, F))).then_inc(const_in, 16)
            sp.dma_start(al_sb[:], alpha.unsqueeze(0).broadcast_to((P, 1))).then_inc(const_in, 16)
            sp.dma_start(w1t_sb[:], w1t).then_inc(const_in, 16)
            load_adj(Batch(0, 0), into_used=False)
            load_x(Batch(0, 1), into_used=False)
            load_adj(Batch(0, 1), into_used=False)
            looped(sp, step)

        @block.gpsimd
        def _(pool):
            start_counts(pool, "pool")
            nc.gpsimd.memset(half_sb[:], -0.5).then_inc(half_ready, 1)
            pool.wait_ge(half_ready, 1)

            def add_bias(t):
                pool.wait_ge(x_in[t.slot], 16 * t.use + 16)
                pool.wait_ge(x1_ready, t.count(1, 1 - SLOTS))
                nc.gpsimd.tensor_tensor(xb_sb[t.slot][:], x_sb[t.slot][:],
                                        bw_sb[:].unsqueeze(1).broadcast_to((P, T, F)), ALU.add).then_inc(xb_ready, 1)

            def rstd1(t):
                pool.wait_ge(v1_ready, t.count(1, 1))
                pool.wait_ge(w_ready, t.count(1, 1 - SLOTS))
                nc.gpsimd.tensor_tensor(rs1_sb[t.slot][:], v1_sb[t.slot][:], half_sb[:], ALU.pow).then_inc(rs1_ready, 1)

            def rstd2(t):
                pool.wait_ge(v2_ready, t.count(1, 1))
                nc.gpsimd.tensor_tensor(rs2_sb[t.slot][:], v2_sb[t.slot][:], half_sb[:], ALU.pow).then_inc(rs2_ready, 1)
                pool.wait_ge(rs2_ready, t.count(1, 1))
                nc.gpsimd.tensor_tensor(nb2_sb[t.slot][:], nm2_sb[t.slot][:], rs2_sb[t.slot][:], ALU.mult).then_inc(nb2_ready, 1)

            def add_residual(t):
                pool.wait_ge(pn_ready, t.count(2, 1))
                pool.wait_ge(out_ready, t.count(1))
                nc.gpsimd.tensor_tensor(px_sb[:], pos_sb[:], x1_sb[t.slot][:], ALU.add).then_inc(px_ready, 1)

            def lower_part(t, half):
                blocks = slice(HT * half, HT * (half + 1))
                pool.wait_ge(hi_ready, t.count(2, half + 1))
                nc.gpsimd.tensor_tensor(lo_sb[t.slot][:, blocks, :], h2_sb[:, blocks, :], hi_sb[t.slot][:, blocks, :],
                                        ALU.subtract).then_inc(lo_ready, 1)

            def step(k, j):
                rstd1(Batch(k, j + 2))
                add_bias(Batch(k, j + 2))
                rstd2(Batch(k, j + 1))
                add_residual(Batch(k, j))
                lower_part(Batch(k, j + 1), 0)
                lower_part(Batch(k, j + 1), 1)

            pool.wait_ge(const_in, CONSTS)
            rstd1(Batch(0, 0))
            add_bias(Batch(0, 0))
            rstd1(Batch(0, 1))
            add_bias(Batch(0, 1))
            rstd2(Batch(0, 0))
            lower_part(Batch(0, 0), 0)
            lower_part(Batch(0, 0), 1)
            looped(pool, step)
            rstd2(Batch(0, 7))
            lower_part(Batch(0, 7), 0)
            lower_part(Batch(0, 7), 1)
            add_residual(Batch(0, 6))
            add_residual(Batch(0, 7))

        @block.vector
        def _(dve):
            tt, ts, stt = nc.vector.tensor_tensor, nc.vector.tensor_scalar, nc.vector.scalar_tensor_tensor

            def set_up():
                n = [0]

                def then(ins):
                    n[0] += 1
                    ins.then_inc(setup, 1)

                def settle():
                    dve.wait_ge(setup, n[0])

                then(nc.vector.memset(ones_sb[:], 1.0))
                then(nc.vector.memset(b1p_sb[:], 0.0))
                then(nc.vector.memset(quarter_sb[:], 0.0))
                settle()
                for q in range(0, P, 32):
                    then(nc.vector.memset(quarter_sb[q:q + 1, :], 1.0))
                dve.wait_ge(const_in, CONSTS)
                nc.vector.tensor_copy(ab_sb[:, 0, :], a_sb[:, 1:2].broadcast_to((P, P))).then_inc(ab_ready, 1)
                nc.vector.tensor_copy(ab_sb[:, 1, :], a_sb[:, 0:1].broadcast_to((P, P))).then_inc(ab_ready, 1)
                then(ts(nal_sb[:], al_sb[:], -1.0, None, ALU.mult))
                then(nc.vector.tensor_copy(b1h_sb[:, 0, :], b1_sb[:]))
                settle()
                then(tt(b1r_sb[:, 0, :], b1_sb[:], b1h_sb[:, 0, :], ALU.subtract))
                settle()
                then(nc.vector.tensor_copy(b1h_sb[:, 1, :], b1r_sb[:, 0, :]))
                settle()
                then(tt(b1r_sb[:, 1, :], b1r_sb[:, 0, :], b1h_sb[:, 1, :], ALU.subtract))
                settle()
                for q, part in ((0, b1h_sb[0:1, 0, :]), (32, b1h_sb[32:33, 1, :]), (64, b1r_sb[64:65, 1, :])):
                    then(nc.vector.tensor_copy(b1p_sb[q:q + 1, :, :], part.unsqueeze(1).broadcast_to((1, HT, F))))
                dve.wait_ge(wa_done, 1)
                nc.vector.tensor_copy(wa_sb[:].rearrange("p i f -> p (i f)"), S[:, 0:2 * F]).then_inc(wa_ready, 1)
                return n[0]

            def statistics(t, layer, src, st, nm, v, step_sem, per, nm_ready, v_ready, scale):
                sm, df, d2, vv = sm_sb[:, layer], df_sb[:, layer], d2_sb[:, layer], vv_sb[:, layer]
                for u in range(T):
                    ins = nc.vector.bn_stats(st[:, u, :], src[:, u, :])
                ins.then_inc(step_sem, 1)
                dve.wait_ge(step_sem, t.count(per, 1))
                tt(sm, st[:, :, 1:3], st[:, :, 4:6], ALU.add).then_inc(step_sem, 1)
                tt(df, st[:, :, 1], st[:, :, 4], ALU.subtract).then_inc(step_sem, 1)
                dve.wait_ge(step_sem, t.count(per, 2))
                ts(nm, sm[:, :, 0], -0.5, None, ALU.mult).then_inc(nm_ready, 1)
                dve.wait_ge(step_sem, t.count(per, 3))
                tt(d2, df, df, ALU.mult).then_inc(step_sem, 1)
                dve.wait_ge(step_sem, t.count(per, 4))
                stt(vv, d2, F / 4.0, sm[:, :, 1], ALU.mult, ALU.add).then_inc(step_sem, 1)
                dve.wait_ge(step_sem, t.count(per, 5))
                ts(v, vv, scale / F, EPS * scale, ALU.mult, ALU.add).then_inc(v_ready, 1)

            def front(t):
                dve.wait_ge(x_in[t.slot], 16 * t.use + 16)
                statistics(t, 0, x_sb[t.slot], st1_sb, nm1_sb[t.slot][:], v1_sb[t.slot][:],
                           front_step, FRONT, nm1_ready, v1_ready, 1.0)

            def dots(t, i):
                for u in range(T):
                    ins = stt(prod_sb[:, u, :], r1_sb[t.slot][:, u, :], 1.0, wa_sb[:, i, :],
                              ALU.mult, ALU.mult, accum_out=dots_sb[:, i, u:u + 1])
                ins.then_inc(dots_step, 1)

            def row_exponents(t):
                dve.wait_ge(r1_ready, t.count(1, 1))
                dots(t, 0)
                dve.wait_ge(rs1_ready, t.count(1, 1))
                dve.wait_ge(dots_step, t.count(DOTS, 1))
                tt(s_sb[:, 0, :], dots_sb[:, 0, :], rs1_sb[t.slot][:], ALU.mult).then_inc(si_ready, 1)

            def column_exponents(t):
                dots(t, 1)
                dve.wait_ge(dots_step, t.count(DOTS, 2))
                tt(sj_sb[:], dots_sb[:, 1, :], rs1_sb[t.slot][:], ALU.mult).then_inc(dots_step, 1)
                dve.wait_ge(dots_step, t.count(DOTS, 3))
                tt(s_sb[:, 1, :], sj_sb[:], ba_sb[:], ALU.add).then_inc(sj_ready, 1)

            def e_parts(t):
                dve.wait_ge(ei_ready, t.count(1, 1))
                e, e_hi = e3_sb[t.slot], e3_hi[t.slot]
                tt(e[:, :, 1], e[:, :, 0], e_hi[:, :, 0], ALU.subtract).then_inc(e_step, 1)
                dve.wait_ge(e_step, t.count(ESPLIT, 1))
                tt(e[:, :, 2], e[:, :, 1], e_hi[:, :, 1], ALU.subtract).then_inc(e_ready, 1)

            def column_weights(t):
                dve.wait_ge(ej_ready, t.count(1, 1))
                stt(w_sb[t.slot][:], ej_sb[t.slot][:], 0.0, rs1_sb[t.slot][:], ALU.not_equal, ALU.mult).then_inc(w_ready, 1)

            def g_parts(t):
                dve.wait_ge(r_done, t.count(1, 1))
                r, div, inv, keep = (gv_sb[:, i, :] for i in range(4))
                g, g_hi = g3_sb[t.slot], g3_hi[t.slot]
                nc.vector.tensor_reduce(r, R[:, 0:4 * T].rearrange("p (u c) -> p u c", c=4)[:, :, 0:PARTS],
                                        AX_X, ALU.add).then_inc(r_read, 1)
                dve.wait_ge(r_read, t.count(1, 1))
                stt(div, r, 0.0, r, ALU.is_equal, ALU.add).then_inc(g_step, 1)
                dve.wait_ge(g_step, t.count(GSPLIT, 1))
                nc.vector.reciprocal(inv, div).then_inc(g_step, 1)
                column_weights(t)
                dve.wait_ge(g_step, t.count(GSPLIT, 2))
                stt(keep, r, 0.0, inv, ALU.not_equal, ALU.mult).then_inc(g_step, 1)
                dve.wait_ge(g_step, t.count(GSPLIT, 3))
                tt(g[:, :, 0], keep, e3_sb[t.slot][:, :, 0], ALU.mult).then_inc(g_step, 1)
                dve.wait_ge(g_step, t.count(GSPLIT, 4))
                tt(g[:, :, 1], g[:, :, 0], g_hi[:, :, 0], ALU.subtract).then_inc(g_step, 1)
                dve.wait_ge(g_step, t.count(GSPLIT, 5))
                tt(g[:, :, 2], g[:, :, 1], g_hi[:, :, 1], ALU.subtract).then_inc(g_ready, 1)

            def add_attention(t):
                dve.wait_ge(q_done, t.count(1, 1))
                nc.vector.tensor_reduce(q_sb[:], Q[:, 0:4 * T].rearrange("p (u c) -> p u c", c=4)[:, :, 0:PARTS],
                                        AX_X, ALU.add).then_inc(q_read, 1)
                dve.wait_ge(q_read, t.count(1, 1))
                dve.wait_ge(ssb_ready, t.count(1, 1))
                dve.wait_ge(xb_ready, t.count(1, 1))
                for u in range(T):
                    ins = stt(x1_sb[t.slot][:, u, :], ssb_sb[:], q_sb[:, u:u + 1], xb_sb[t.slot][:, u, :],
                              ALU.mult, ALU.add)
                ins.then_inc(x1_ready, 1)

            def middle(t):
                dve.wait_ge(x1_ready, t.count(1, 1))
                statistics(t, 1, x1_sb[t.slot], st2_sb, nm2_sb[t.slot][:], v2_sb[t.slot][:],
                           back_step, FRONT, nm2_ready, v2_ready, H_SCALE ** -2)

            def finish(t):
                dve.wait_ge(px_ready, t.count(1, 1))
                dve.wait_ge(pn_ready, t.count(2, 2))
                dve.wait_ge(out_stored[t.slot], 16 * t.use + START)
                stt(out_sb[t.slot][:], neg_sb[:], nal_sb[:], px_sb[:], ALU.mult, ALU.add).then_inc(out_ready, 1)

            def step(k, j):
                front(Batch(k, j + 2))
                add_attention(Batch(k, j + 1))
                middle(Batch(k, j + 1))
                row_exponents(Batch(k, j + 2))
                e_parts(Batch(k, j + 2))
                column_exponents(Batch(k, j + 2))
                g_parts(Batch(k, j + 2))
                finish(Batch(k, j))

            start_counts(dve, "dve")
            nc.vector.memset(zero_sb[:], 0.0).then_inc(zero_ready, 1)
            front(Batch(0, 0))
            n_setup = set_up()
            dve.wait_ge(setup, n_setup)
            dve.wait_ge(wa_ready, 1)
            row_exponents(Batch(0, 0))
            e_parts(Batch(0, 0))
            column_exponents(Batch(0, 0))
            g_parts(Batch(0, 0))
            front(Batch(0, 1))
            add_attention(Batch(0, 0))
            middle(Batch(0, 0))
            row_exponents(Batch(0, 1))
            e_parts(Batch(0, 1))
            column_exponents(Batch(0, 1))
            g_parts(Batch(0, 1))
            looped(dve, step)
            add_attention(Batch(0, 7))
            middle(Batch(0, 7))
            finish(Batch(0, 6))
            finish(Batch(0, 7))

        @block.scalar
        def _(act):
            def relu_centred(t):
                act.wait_ge(x_in[t.slot], 16 * t.use + 16)
                act.wait_ge(nm1_ready, t.count(1, 1))
                act.wait_ge(hs_done, t.count(1, 1 - SLOTS))
                for u in range(T):
                    ins = nc.scalar.activation(r1_sb[t.slot][:, u, :], x_sb[t.slot][:, u, :], ACT.Relu,
                                               bias=nm1_sb[t.slot][:, u:u + 1])
                ins.then_inc(r1_ready, 1)

            def row_exponentials(t):
                act.wait_ge(si_ready, t.count(1, 1))
                nc.scalar.activation(e3_sb[t.slot][:, :, 0], s_sb[:, 0, :], ACT.Exp).then_inc(ei_ready, 1)

            def column_exponentials(t):
                act.wait_ge(sj_ready, t.count(1, 1))
                nc.scalar.activation(ej_sb[t.slot][:], s_sb[:, 1, :], ACT.Exp).then_inc(ej_ready, 1)

            def normalise(t, half):
                act.wait_ge(nb2_ready, t.count(1, 1))
                act.wait_ge(lo_ready, t.count(2, 0))
                for u in range(HT * half, HT * (half + 1)):
                    ins = nc.scalar.activation(h2_sb[:, u, :], x1_sb[t.slot][:, u, :], ACT.Relu,
                                               scale=rs2_sb[t.slot][:, u:u + 1], bias=nb2_sb[t.slot][:, u:u + 1])
                ins.then_inc(h2_ready, 1)

            def upper_part(t, half):
                blocks = slice(HT * half, HT * (half + 1))
                act.wait_ge(h2_ready, t.count(2, half + 1))
                nc.scalar.activation(hi_sb[t.slot][:, blocks, :], h2_sb[:, blocks, :], ACT.Copy).then_inc(hi_ready, 1)

            def copy_product(t, h):
                act.wait_ge(y_done, t.count(2))
                act.wait_ge(gt_done, t.count(2, h + 1))
                nc.scalar.activation(gt_sb[:, 512 * h:512 * (h + 1)], GT[:, h, :], ACT.Copy,
                                     scale=1.0 / H_SCALE).then_inc(gt_ready, 1)

            y = Y[:].rearrange("p h (u f) -> p (h u) f", f=F)

            def positive(t):
                act.wait_ge(y_done, t.count(2, 2))
                act.wait_ge(px_ready, t.count(1))
                nc.scalar.activation(pos_sb[:], y, ACT.Relu).then_inc(pn_ready, 1)

            def negative(t):
                act.wait_ge(out_ready, t.count(1))
                nc.scalar.activation(neg_sb[:], y, ACT.Relu, scale=-1.0).then_inc(pn_ready, 1)

            def copy_sum(t):
                act.wait_ge(hs_done, t.count(1, 1))
                act.wait_ge(turned, t.count(1))
                nc.scalar.activation(hr_sb[:], HS[:, 0:F], ACT.Copy).then_inc(hr_ready, 1)

            def spread_sum(t):
                act.wait_ge(turned, t.count(1, 1))
                nc.scalar.activation(hsb_sb[:], S[:, F:2 * F], ACT.Copy).then_inc(hsb_ready, 1)

            def keep_sum(t):
                act.wait_ge(s_done, t.count(1, 1))
                act.wait_ge(x1_ready, t.count(1))
                nc.scalar.activation(ssb_sb[:], S[:, 0:F], ACT.Copy).then_inc(ssb_ready, 1)

            def store(t):
                act.wait_ge(out_ready, t.count(1, 1))
                act.dma_start(out_d[t.index], out_sb[t.slot][:].rearrange("p t f -> p (t f)")).then_inc(out_stored[t.slot], 16)

            def step(k, j):
                relu_centred(Batch(k, j + 2))
                copy_product(Batch(k, j), 0)
                copy_product(Batch(k, j), 1)
                row_exponentials(Batch(k, j + 2))
                normalise(Batch(k, j + 1), 0)
                positive(Batch(k, j))
                column_exponentials(Batch(k, j + 2))
                upper_part(Batch(k, j + 1), 0)
                negative(Batch(k, j))
                copy_sum(Batch(k, j + 2))
                normalise(Batch(k, j + 1), 1)
                spread_sum(Batch(k, j + 2))
                upper_part(Batch(k, j + 1), 1)
                keep_sum(Batch(k, j + 2))
                store(Batch(k, j))

            act.dma_start(a_sb[:], a).then_inc(const_in, 16)
            act.dma_start(w0t_sb[:], w0t).then_inc(const_in, 16)
            act.dma_start(b1_sb[:], bias1.unsqueeze(0).broadcast_to((P, F))).then_inc(const_in, 16)
            act.dma_start(ba_sb[:], bias_a.rearrange("(p t) -> p t", t=T)).then_inc(const_in, 16)
            act.wait_ge(zero_ready, 1)
            nc.scalar.activation(warm_sb[:], zero_sb[:], ACT.Exp).then_inc(warmed, 1)
            start_counts(act, "act")
            relu_centred(Batch(0, 0))
            row_exponentials(Batch(0, 0))
            column_exponentials(Batch(0, 0))
            copy_sum(Batch(0, 0))
            spread_sum(Batch(0, 0))
            keep_sum(Batch(0, 0))
            relu_centred(Batch(0, 1))
            row_exponentials(Batch(0, 1))
            normalise(Batch(0, 0), 0)
            column_exponentials(Batch(0, 1))
            upper_part(Batch(0, 0), 0)
            copy_sum(Batch(0, 1))
            normalise(Batch(0, 0), 1)
            spread_sum(Batch(0, 1))
            upper_part(Batch(0, 0), 1)
            keep_sum(Batch(0, 1))
            looped(act, step)
            copy_product(Batch(0, 6), 0)
            copy_product(Batch(0, 6), 1)
            normalise(Batch(0, 7), 0)
            upper_part(Batch(0, 7), 0)
            normalise(Batch(0, 7), 1)
            upper_part(Batch(0, 7), 1)
            positive(Batch(0, 6))
            negative(Batch(0, 6))
            store(Batch(0, 6))
            copy_product(Batch(0, 7), 0)
            copy_product(Batch(0, 7), 1)
            positive(Batch(0, 7))
            negative(Batch(0, 7))
            store(Batch(0, 7))
            for s in range(SLOTS):
                act.wait_ge(out_stored[s], 16 * len(range(s, B, SLOTS)) + START)

        @block.tensor
        def _(pe):
            mm = nc.tensor.matmul

            def set_up():
                pe.wait_ge(const_in, CONSTS)
                for i in range(2):
                    pe.wait_ge(ab_ready, i + 1)
                    ins = mm(S[:, F * i:F * (i + 1)], ab_sb[:, i, :], w0t_sb[:], start=True, stop=True)
                ins.then_inc(wa_done, 1)

            def times_adj(bank, parts, t, done, chunks):
                for u in range(T):
                    if chunks and u % UC == 0:
                        pe.wait_ge(adj_in[t.slot][u // UC], 16 * t.use + 16)
                    for c in range(T):
                        ins = mm(bank[:, 4 * u:4 * u + PARTS], adj_hi[t.slot][:, u, c, :], parts[t.slot][:, c, :],
                                 start=(c == 0), stop=(c == T - 1))
                ins.then_inc(done, 1)

            def row_sums(t):
                pe.wait_ge(e_ready, t.count(1, 1))
                pe.wait_ge(r_read, t.count(1))
                times_adj(R, e3_hi, t, r_done, True)

            def column_sums(t):
                pe.wait_ge(w_ready, t.count(1, 1))
                pe.wait_ge(hr_ready, t.count(1))
                for u in range(T):
                    q = 32 * (u % 4)
                    ins = mm(HS[q:q + 32, 0:F], w_sb[t.slot][:, u:u + 1].broadcast_to((P, 32)), r1_sb[t.slot][:, u, :],
                             start=(u < 4), stop=(u >= T - 4))
                ins.then_inc(hs_done, 1)

            def turn_sum(t):
                pe.wait_ge(hr_ready, t.count(1, 1))
                pe.wait_ge(ssb_ready, t.count(1))
                mm(S[:, F:2 * F], hr_sb[:], quarter_sb[:], start=True, stop=True).then_inc(turned, 1)

            def spread_projection(t):
                pe.wait_ge(hsb_ready, t.count(1, 1))
                mm(S[:, 0:F], hsb_sb[:], w0_sb[:], start=True, stop=True).then_inc(s_done, 1)

            def weighted(t):
                pe.wait_ge(g_ready, t.count(1, 1))
                pe.wait_ge(q_read, t.count(1))
                times_adj(Q, g3_hi, t, q_done, False)

            def product(t, h, blocks):
                if 0 in blocks:
                    pe.wait_ge(gt_ready, t.count(2))
                for c in blocks:
                    if c % HT == 0 or c == blocks[0]:
                        pe.wait_ge(lo_ready, t.count(2, c // HT + 1))
                    for part in (hi_sb, lo_sb):
                        ins = mm(GT[:, h, :], part[t.slot][:, c, :], adj_hi[t.slot][:, HT * h:HT * (h + 1), c, :],
                                 start=(c == 0 and part is hi_sb), stop=(c == T - 1 and part is lo_sb))
                if T - 1 in blocks:
                    ins.then_inc(gt_done, 1)

            def project(t, h):
                pe.wait_ge(pn_ready, t.count(2))
                mm(Y[:, h, :], ones_sb[:], b1p_sb[:].rearrange("p u f -> p (u f)"), start=True, stop=False)
                pe.wait_ge(gt_ready, t.count(2, h + 1))
                for u in range(HT):
                    at = HT * h + u
                    ins = mm(Y[:, h, F * u:F * (u + 1)], gt_sb[:, P * at:P * (at + 1)], w1t_sb[:],
                             start=False, stop=(u == HT - 1))
                ins.then_inc(y_done, 1)

            def step(k, j):
                row_sums(Batch(k, j + 1))
                column_sums(Batch(k, j + 1))
                weighted(Batch(k, j + 1))
                turn_sum(Batch(k, j + 1))
                product(Batch(k, j), 0, range(0, 2))
                spread_projection(Batch(k, j + 1))
                product(Batch(k, j), 0, range(2, T))
                product(Batch(k, j), 1, range(T))
                project(Batch(k, j), 0)
                project(Batch(k, j), 1)

            start_counts(pe, "pe")
            set_up()
            row_sums(Batch(0, 0))
            column_sums(Batch(0, 0))
            weighted(Batch(0, 0))
            turn_sum(Batch(0, 0))
            spread_projection(Batch(0, 0))
            looped(pe, step)
            row_sums(Batch(0, 7))
            column_sums(Batch(0, 7))
            weighted(Batch(0, 7))
            turn_sum(Batch(0, 7))
            product(Batch(0, 6), 0, range(0, 2))
            spread_projection(Batch(0, 7))
            product(Batch(0, 6), 0, range(2, T))
            product(Batch(0, 6), 1, range(T))
            project(Batch(0, 6), 0)
            project(Batch(0, 6), 1)
            for h in range(2):
                product(Batch(0, 7), h, range(T))
            for h in range(2):
                project(Batch(0, 7), h)


def kernel(x, adj, L0_gnn_W, L0_gnn_a, L0_gnn_bias_a, L0_gnn_bias_W, L1_gnn_W, L1_gnn_bias, L1_gnn_prelu_a):
    import numpy as np
    import concourse.bacc as bacc
    from concourse.bass_utils import run_bass_kernel_spmd

    B, N, F = x.shape
    T = N // P
    arrays = {
        "x": np.asarray(x),
        "adj": np.asarray(adj).reshape(B, P, T, P, T).transpose(0, 3, 2, 4, 1),
        "w0": np.asarray(L0_gnn_W),
        "w0t": np.asarray(L0_gnn_W).T,
        "a": np.asarray(L0_gnn_a).reshape(2, F).T,
        "bias_a": np.asarray(L0_gnn_bias_a),
        "bias_w": np.asarray(L0_gnn_bias_W),
        "w1t": np.asarray(L1_gnn_W).T,
        "bias1": np.asarray(L1_gnn_bias),
        "alpha": np.asarray(L1_gnn_prelu_a),
    }
    arrays = {name: np.ascontiguousarray(v) for name, v in arrays.items()}
    nc = bacc.Bacc("TRN2", target_bir_lowering=False, num_devices=1)
    args = [nc.dram_tensor(name, v.shape, mybir.dt.from_np(v.dtype), kind="ExternalInput").ap() for name, v in arrays.items()]
    args.append(nc.dram_tensor("out", (B, N, F), F32, kind="ExternalOutput").ap())
    build(nc, *args)
    result = run_bass_kernel_spmd(nc, [arrays], core_ids=[0])
    return result.results[0]["out"]
```

```python
from contextlib import ExitStack

import concourse.bass as bass
from concourse import mybir

F32 = mybir.dt.float32
BF16 = mybir.dt.bfloat16
F16 = mybir.dt.float16
ALU = mybir.AluOpType
ACT = mybir.ActivationFunctionType
AX_X = mybir.AxisListType.X

P = 128
SLOTS = 3
CHUNKS = 4
PARTS = 3
H_SCALE = 4096.0
EPS = 1e-5

PROJ = 16 * 2
CONSTS = 16 * 2
LATE = 16 * 2
WEIGHTS = 16 * 2
START = 2
FRONT, BACK, DOTS, ESPLIT, GSPLIT = 3, 5, 3, 1, 5


class Batch:

    def __init__(self, k, d):
        self.index = SLOTS * k + d
        self.slot = d % SLOTS
        self.use = k + d // SLOTS
        self.k, self.d = k, d

    def count(self, per, n=0):
        at_first_turn = per * self.d + n + START
        if isinstance(self.k, int):
            return max(per * SLOTS * self.k + at_first_turn, START)
        assert at_first_turn > 0
        return (per * SLOTS) * self.k + at_first_turn


def build(nc, x, adj, w0, w0t, a, bias_a, bias_w, w1t, bias1, alpha, out):
    B, N, F = x.shape
    T = N // P
    HT = T // 2
    UC = T // CHUNKS
    assert B == 8 and F == P and HT * F == 512

    x_d = x.rearrange("b (p t) f -> b p (t f)", t=T)
    out_d = out.rearrange("b (p t) f -> b p (t f)", t=T)

    with ExitStack() as ctx:
        def sb(name, shape, dt=F32):
            return ctx.enter_context(nc.sbuf_tensor(name, shape, dt))

        def ring(name, shape, dt=F32):
            return [sb(f"{name}{s}", shape, dt) for s in range(SLOTS)]

        def psum(name, shape):
            return ctx.enter_context(nc.psum_tensor(name, shape, F32))

        def sem(name):
            return ctx.enter_context(nc.semaphore(name))

        raisers = {"dve": [], "pool": [], "act": [], "pe": []}

        def counted(name, by):
            raisers[by].append(sem(name))
            return raisers[by][-1]

        def start_counts(eng, by):
            for each in raisers[by]:
                eng.sem_inc(each, START)

        def upper(words, dims, **sizes):
            halves = words.rearrange(f"p {dims} -> p ({dims})").bitcast(BF16)
            return halves.rearrange(f"p ({dims} h) -> p {dims} h", h=2, **sizes)[(slice(None),) * (len(sizes) + 2) + (1,)]

        adj_sb = ring("adj_sb", [P, T, T, P])
        adj_hi = [upper(s[:], "u t q", u=T, t=T) for s in adj_sb]
        x_sb = ring("x_sb", [P, T, F])
        xb_sb = ring("xb_sb", [P, T, F])
        r1_sb = ring("r1_sb", [P, T, F])
        x1_sb = ring("x1_sb", [P, T, F])
        hi_sb = ring("hi_sb", [P, T, F], F16)
        lo_sb = ring("lo_sb", [P, T, F], F16)
        out_sb = ring("out_sb", [P, T, F])
        e3_sb = ring("e3_sb", [P, T, PARTS])
        g3_sb = ring("g3_sb", [P, T, PARTS])
        e3_hi = [upper(s[:], "t c", t=T) for s in e3_sb]
        g3_hi = [upper(s[:], "t c", t=T) for s in g3_sb]
        ej_sb = ring("ej_sb", [P, T])
        w_sb = ring("w_sb", [P, T])
        nm1_sb = ring("nm1_sb", [P, T])
        nm2_sb = ring("nm2_sb", [P, T])
        v1_sb = ring("v1_sb", [P, T])
        v2_sb = ring("v2_sb", [P, T])
        rs1_sb = ring("rs1_sb", [P, T])
        rs2_sb = ring("rs2_sb", [P, T])
        nb2_sb = ring("nb2_sb", [P, T])

        h2_sb = sb("h2_sb", [P, T, F])
        gt_sb = sb("gt_sb", [P, T * P])
        pos_sb = sb("pos_sb", [P, T, F])
        neg_sb = sb("neg_sb", [P, T, F])
        px_sb = sb("px_sb", [P, T, F])
        hr_sb = sb("hr_sb", [P, F])
        hsb_sb = sb("hsb_sb", [P, P])
        quarter_sb = sb("quarter_sb", [P, P])
        ssb_sb = sb("ssb_sb", [P, F])
        prod_sb = sb("prod_sb", [P, T, F])
        dots_sb = sb("dots_sb", [P, 2, T])
        s_sb = sb("s_sb", [P, 2, T])
        sj_sb = sb("sj_sb", [P, T])
        st1_sb = sb("st1_sb", [P, T, 6])
        st2_sb = sb("st2_sb", [P, T, 6])
        sm_sb = sb("sm_sb", [P, 2, T, 2])
        df_sb = sb("df_sb", [P, 2, T])
        d2_sb = sb("d2_sb", [P, T])
        vv_sb = sb("vv_sb", [P, T])
        vp_sb = sb("vp_sb", [P, 2, T])
        gv_sb = sb("gv_sb", [P, 4, T])
        q_sb = sb("q_sb", [P, T])

        w0_sb = sb("w0_sb", [P, F])
        w0t_sb = sb("w0t_sb", [P, F])
        w1t_sb = sb("w1t_sb", [P, F])
        a_sb = sb("a_sb", [P, 2])
        ab_sb = sb("ab_sb", [P, 2, P])
        wa_sb = sb("wa_sb", [P, 2, F])
        ba_sb = sb("ba_sb", [P, T])
        bw_sb = sb("bw_sb", [P, F])
        b1_sb = sb("b1_sb", [P, F])
        b1r_sb = sb("b1r_sb", [P, 2, F])
        b1p_sb = sb("b1p_sb", [P, HT, F], BF16)
        b1h_sb = sb("b1h_sb", [P, 2, F], BF16)
        ones_sb = sb("ones_sb", [P, P], BF16)
        al_sb = sb("al_sb", [P, 1])
        nal_sb = sb("nal_sb", [P, 1])
        zero_sb = sb("zero_sb", [P, 1])
        warm_sb = sb("warm_sb", [P, 1])
        half_sb = sb("half_sb", [P, T])

        GT = psum("GT", [P, 2, 512])
        Y = psum("Y", [P, 2, 512])
        HS = psum("HS", [P, 512])
        S = psum("S", [P, 512])
        R = psum("R", [P, 512])
        Q = psum("Q", [P, 512])

        proj_in = sem("proj_in")
        const_in = sem("const_in")
        late_in = sem("late_in")
        weights_in = sem("weights_in")
        x_in = [sem(f"x_in{s}") for s in range(SLOTS)]
        adj_in = [[sem(f"adj_in{s}_{c}") for c in range(CHUNKS)] for s in range(SLOTS)]
        out_stored = [counted(f"out_stored{s}", "act") for s in range(SLOTS)]
        ab_ready = sem("ab_ready")
        wa_done = sem("wa_done")
        wa_ready = sem("wa_ready")
        setup = sem("setup")
        half_ready = sem("half_ready")
        zero_ready = sem("zero_ready")
        warmed = sem("warmed")
        front_step = counted("front_step", "dve")
        nm1_ready = counted("nm1_ready", "dve")
        dots_step = counted("dots_step", "dve")
        si_ready = counted("si_ready", "dve")
        sj_ready = counted("sj_ready", "dve")
        e_step = counted("e_step", "dve")
        e_ready = counted("e_ready", "dve")
        w_ready = counted("w_ready", "dve")
        r_read = counted("r_read", "dve")
        g_step = counted("g_step", "dve")
        g_ready = counted("g_ready", "dve")
        q_read = counted("q_read", "dve")
        x1_ready = counted("x1_ready", "dve")
        back_step = counted("back_step", "dve")
        nm2_ready = counted("nm2_ready", "dve")
        v2_ready = counted("v2_ready", "dve")
        px_ready = counted("px_ready", "dve")
        xb_ready = counted("xb_ready", "pool")
        v1_ready = counted("v1_ready", "pool")
        rs1_ready = counted("rs1_ready", "pool")
        rs2_ready = counted("rs2_ready", "pool")
        nb2_ready = counted("nb2_ready", "pool")
        lo_ready = counted("lo_ready", "pool")
        out_ready = counted("out_ready", "pool")
        spread_ready = counted("spread_ready", "act")
        r1_ready = counted("r1_ready", "act")
        ei_ready = counted("ei_ready", "act")
        ej_ready = counted("ej_ready", "act")
        h2_ready = counted("h2_ready", "act")
        hi_ready = counted("hi_ready", "act")
        gt_ready = counted("gt_ready", "act")
        pos_ready = counted("pos_ready", "act")
        neg_ready = counted("neg_ready", "act")
        hr_ready = counted("hr_ready", "act")
        hsb_ready = counted("hsb_ready", "act")
        ssb_ready = counted("ssb_ready", "act")
        r_done = counted("r_done", "pe")
        hs_done = counted("hs_done", "pe")
        turned = counted("turned", "pe")
        s_done = counted("s_done", "pe")
        q_done = counted("q_done", "pe")
        gt_done = counted("gt_done", "pe")
        y_done = counted("y_done", "pe")

        def looped(eng, step):
            with eng.Fori(0, (B - 2) // SLOTS) as k:
                for j in range(SLOTS):
                    step(k, j)

        block = ctx.enter_context(nc.Block())

        @block.sync
        def _(sp):
            def load_x(t, into_used=True):
                if into_used:
                    sp.wait_ge(r1_ready, t.count(1, 1 - SLOTS))
                    sp.wait_ge(xb_ready, t.count(1, 1 - SLOTS))
                sp.dma_start(x_sb[t.slot][:].rearrange("p t f -> p (t f)"), x_d[t.index]).then_inc(x_in[t.slot], 16)

            def load_adj(t, into_used=True):
                for c in range(CHUNKS):
                    if into_used and c % (CHUNKS // 2) == 0:
                        sp.wait_ge(gt_done, t.count(2, 2 * c // CHUNKS + 1 - 2 * SLOTS))
                    sp.dma_start(adj_sb[t.slot][:, UC * c:UC * (c + 1), :, :].rearrange("p u t q -> p (u t q)"),
                                 adj[t.index, :, UC * c:UC * (c + 1), :, :].rearrange("p u t q -> p (u t q)")
                                 ).then_inc(adj_in[t.slot][c], 16)

            def step(k, j):
                load_x(Batch(k, j + 2))
                load_adj(Batch(k, j + 2))

            load_x(Batch(0, 0), into_used=False)
            sp.dma_start(bw_sb[:], bias_w.unsqueeze(0).broadcast_to((P, F))).then_inc(const_in, 16)
            sp.dma_start(b1_sb[:], bias1.unsqueeze(0).broadcast_to((P, F))).then_inc(late_in, 16)
            load_adj(Batch(0, 0), into_used=False)
            load_x(Batch(0, 1), into_used=False)
            load_adj(Batch(0, 1), into_used=False)
            looped(sp, step)

        @block.gpsimd
        def _(pool):
            pool.dma_start(w0_sb[:], w0).then_inc(weights_in, 16)
            pool.dma_start(w1t_sb[:], w1t).then_inc(weights_in, 16)
            start_counts(pool, "pool")
            nc.gpsimd.memset(half_sb[:], -0.5).then_inc(half_ready, 1)
            pool.wait_ge(half_ready, 1)

            def add_bias(t):
                pool.wait_ge(x_in[t.slot], 16 * t.use + 16)
                pool.wait_ge(x1_ready, t.count(1, 1 - SLOTS))
                nc.gpsimd.tensor_tensor(xb_sb[t.slot][:], x_sb[t.slot][:],
                                        bw_sb[:].unsqueeze(1).broadcast_to((P, T, F)), ALU.add).then_inc(xb_ready, 1)

            def rstd1(t):
                pool.wait_ge(spread_ready, t.count(2, 2))
                nc.gpsimd.tensor_tensor(v1_sb[t.slot][:], vp_sb[:, 0], vp_sb[:, 1], ALU.add).then_inc(v1_ready, 1)
                pool.wait_ge(v1_ready, t.count(1, 1))
                pool.wait_ge(w_ready, t.count(1, 1 - SLOTS))
                nc.gpsimd.tensor_tensor(rs1_sb[t.slot][:], v1_sb[t.slot][:], half_sb[:], ALU.pow).then_inc(rs1_ready, 1)

            def rstd2(t):
                pool.wait_ge(v2_ready, t.count(1, 1))
                nc.gpsimd.tensor_tensor(rs2_sb[t.slot][:], v2_sb[t.slot][:], half_sb[:], ALU.pow).then_inc(rs2_ready, 1)
                pool.wait_ge(rs2_ready, t.count(1, 1))
                nc.gpsimd.tensor_tensor(nb2_sb[t.slot][:], nm2_sb[t.slot][:], rs2_sb[t.slot][:], ALU.mult).then_inc(nb2_ready, 1)

            def finish(t, half):
                blocks = slice(HT * half, HT * (half + 1))
                pool.wait_ge(px_ready, t.count(2, half + 1))
                pool.wait_ge(pos_ready, t.count(2, half + 1))
                if half == 0:
                    pool.wait_ge(out_stored[t.slot], 16 * t.use + START)
                nc.gpsimd.tensor_tensor(out_sb[t.slot][:, blocks, :], px_sb[:, blocks, :], pos_sb[:, blocks, :],
                                        ALU.add).then_inc(out_ready, 1)

            def lower_part(t, half):
                blocks = slice(HT * half, HT * (half + 1))
                pool.wait_ge(hi_ready, t.count(2, half + 1))
                nc.gpsimd.tensor_tensor(lo_sb[t.slot][:, blocks, :], h2_sb[:, blocks, :], hi_sb[t.slot][:, blocks, :],
                                        ALU.subtract).then_inc(lo_ready, 1)

            def step(k, j):
                add_bias(Batch(k, j + 2))
                rstd1(Batch(k, j + 2))
                rstd2(Batch(k, j + 1))
                finish(Batch(k, j), 0)
                lower_part(Batch(k, j + 1), 0)
                finish(Batch(k, j), 1)
                lower_part(Batch(k, j + 1), 1)

            pool.wait_ge(const_in, CONSTS)
            rstd1(Batch(0, 0))
            add_bias(Batch(0, 0))
            rstd1(Batch(0, 1))
            add_bias(Batch(0, 1))
            rstd2(Batch(0, 0))
            lower_part(Batch(0, 0), 0)
            lower_part(Batch(0, 0), 1)
            looped(pool, step)
            rstd2(Batch(0, 7))
            finish(Batch(0, 6), 0)
            finish(Batch(0, 6), 1)

        @block.vector
        def _(dve):
            tt, ts, stt = nc.vector.tensor_tensor, nc.vector.tensor_scalar, nc.vector.scalar_tensor_tensor

            n = [0]

            def then(ins):
                n[0] += 1
                ins.then_inc(setup, 1)

            def settle():
                dve.wait_ge(setup, n[0])

            def set_up():
                then(nc.vector.memset(ones_sb[:], 1.0))
                then(nc.vector.memset(b1p_sb[:], 0.0))
                then(nc.vector.memset(quarter_sb[:], 0.0))
                settle()
                for q in range(0, P, 32):
                    then(nc.vector.memset(quarter_sb[q:q + 1, :], 1.0))
                dve.wait_ge(proj_in, PROJ)
                nc.vector.tensor_copy(ab_sb[:, 0, :], a_sb[:, 1:2].broadcast_to((P, P))).then_inc(ab_ready, 1)
                nc.vector.tensor_copy(ab_sb[:, 1, :], a_sb[:, 0:1].broadcast_to((P, P))).then_inc(ab_ready, 1)
                dve.wait_ge(wa_done, 1)
                nc.vector.tensor_copy(wa_sb[:].rearrange("p i f -> p (i f)"), S[:, 0:2 * F]).then_inc(wa_ready, 1)

            def set_up_bias():
                dve.wait_ge(late_in, LATE)
                then(nc.vector.tensor_copy(b1h_sb[:, 0, :], b1_sb[:]))
                settle()
                then(tt(b1r_sb[:, 0, :], b1_sb[:], b1h_sb[:, 0, :], ALU.subtract))
                settle()
                then(nc.vector.tensor_copy(b1h_sb[:, 1, :], b1r_sb[:, 0, :]))
                settle()
                then(tt(b1r_sb[:, 1, :], b1r_sb[:, 0, :], b1h_sb[:, 1, :], ALU.subtract))
                settle()
                for q, part in ((0, b1h_sb[0:1, 0, :]), (32, b1h_sb[32:33, 1, :]), (64, b1r_sb[64:65, 1, :])):
                    then(nc.vector.tensor_copy(b1p_sb[q:q + 1, :, :], part.unsqueeze(1).broadcast_to((1, HT, F))))
                then(ts(nal_sb[:], al_sb[:], -1.0, None, ALU.mult))
                settle()

            def sums(t, layer, src, st, nm, step_sem, per, nm_ready):
                sm, df = sm_sb[:, layer], df_sb[:, layer]
                for u in range(T):
                    ins = nc.vector.bn_stats(st[:, u, :], src[:, u, :])
                ins.then_inc(step_sem, 1)
                dve.wait_ge(step_sem, t.count(per, 1))
                tt(sm, st[:, :, 1:3], st[:, :, 4:6], ALU.add).then_inc(step_sem, 1)
                tt(df, st[:, :, 1], st[:, :, 4], ALU.subtract).then_inc(step_sem, 1)
                dve.wait_ge(step_sem, t.count(per, 2))
                ts(nm, sm[:, :, 0], -0.5, None, ALU.mult).then_inc(nm_ready, 1)

            def front(t):
                dve.wait_ge(x_in[t.slot], 16 * t.use + 16)
                dve.wait_ge(spread_ready, t.count(2))
                sums(t, 0, x_sb[t.slot], st1_sb, nm1_sb[t.slot][:], front_step, FRONT, nm1_ready)

            def dots(t, i):
                for u in range(T):
                    ins = stt(prod_sb[:, u, :], r1_sb[t.slot][:, u, :], 1.0, wa_sb[:, i, :],
                              ALU.mult, ALU.mult, accum_out=dots_sb[:, i, u:u + 1])
                ins.then_inc(dots_step, 1)

            def row_exponents(t):
                dve.wait_ge(r1_ready, t.count(1, 1))
                dots(t, 0)
                dve.wait_ge(rs1_ready, t.count(1, 1))
                dve.wait_ge(dots_step, t.count(DOTS, 1))
                tt(s_sb[:, 0, :], dots_sb[:, 0, :], rs1_sb[t.slot][:], ALU.mult).then_inc(si_ready, 1)

            def column_exponents(t):
                dots(t, 1)
                dve.wait_ge(dots_step, t.count(DOTS, 2))
                tt(sj_sb[:], dots_sb[:, 1, :], rs1_sb[t.slot][:], ALU.mult).then_inc(dots_step, 1)
                dve.wait_ge(dots_step, t.count(DOTS, 3))
                tt(s_sb[:, 1, :], sj_sb[:], ba_sb[:], ALU.add).then_inc(sj_ready, 1)

            def e_parts(t):
                dve.wait_ge(ei_ready, t.count(1, 1))
                e, e_hi = e3_sb[t.slot], e3_hi[t.slot]
                tt(e[:, :, 1], e[:, :, 0], e_hi[:, :, 0], ALU.subtract).then_inc(e_step, 1)
                dve.wait_ge(e_step, t.count(ESPLIT, 1))
                tt(e[:, :, 2], e[:, :, 1], e_hi[:, :, 1], ALU.subtract).then_inc(e_ready, 1)

            def column_weights(t):
                dve.wait_ge(ej_ready, t.count(1, 1))
                stt(w_sb[t.slot][:], ej_sb[t.slot][:], 0.0, rs1_sb[t.slot][:], ALU.not_equal, ALU.mult).then_inc(w_ready, 1)

            def g_parts(t):
                dve.wait_ge(r_done, t.count(1, 1))
                r, div, inv, keep = (gv_sb[:, i, :] for i in range(4))
                g, g_hi = g3_sb[t.slot], g3_hi[t.slot]
                nc.vector.tensor_reduce(r, R[:, 0:4 * T].rearrange("p (u c) -> p u c", c=4)[:, :, 0:PARTS],
                                        AX_X, ALU.add).then_inc(r_read, 1)
                dve.wait_ge(r_read, t.count(1, 1))
                stt(div, r, 0.0, r, ALU.is_equal, ALU.add).then_inc(g_step, 1)
                dve.wait_ge(g_step, t.count(GSPLIT, 1))
                nc.vector.reciprocal(inv, div).then_inc(g_step, 1)
                dve.wait_ge(g_step, t.count(GSPLIT, 2))
                stt(keep, r, 0.0, inv, ALU.not_equal, ALU.mult).then_inc(g_step, 1)
                dve.wait_ge(g_step, t.count(GSPLIT, 3))
                tt(g[:, :, 0], keep, e3_sb[t.slot][:, :, 0], ALU.mult).then_inc(g_step, 1)
                dve.wait_ge(g_step, t.count(GSPLIT, 4))
                tt(g[:, :, 1], g[:, :, 0], g_hi[:, :, 0], ALU.subtract).then_inc(g_step, 1)
                dve.wait_ge(g_step, t.count(GSPLIT, 5))
                tt(g[:, :, 2], g[:, :, 1], g_hi[:, :, 1], ALU.subtract).then_inc(g_ready, 1)

            def add_attention(t):
                dve.wait_ge(q_done, t.count(1, 1))
                nc.vector.tensor_reduce(q_sb[:], Q[:, 0:4 * T].rearrange("p (u c) -> p u c", c=4)[:, :, 0:PARTS],
                                        AX_X, ALU.add).then_inc(q_read, 1)
                dve.wait_ge(q_read, t.count(1, 1))
                dve.wait_ge(ssb_ready, t.count(1, 1))
                dve.wait_ge(xb_ready, t.count(1, 1))
                for u in range(T):
                    ins = stt(x1_sb[t.slot][:, u, :], ssb_sb[:], q_sb[:, u:u + 1], xb_sb[t.slot][:, u, :],
                              ALU.mult, ALU.add)
                ins.then_inc(x1_ready, 1)

            def middle(t):
                dve.wait_ge(x1_ready, t.count(1, 1))
                sums(t, 1, x1_sb[t.slot], st2_sb, nm2_sb[t.slot][:], back_step, BACK, nm2_ready)
                scale = H_SCALE ** -2
                dve.wait_ge(back_step, t.count(BACK, 3))
                stt(d2_sb[:], df_sb[:, 1], scale / 4.0, df_sb[:, 1], ALU.mult, ALU.mult).then_inc(back_step, 1)
                ts(vv_sb[:], sm_sb[:, 1, :, 1], scale / F, EPS * scale, ALU.mult, ALU.add).then_inc(back_step, 1)
                dve.wait_ge(back_step, t.count(BACK, 5))
                tt(v2_sb[t.slot][:], d2_sb[:], vv_sb[:], ALU.add).then_inc(v2_ready, 1)

            def add_negative(t, half):
                blocks = slice(HT * half, HT * (half + 1))
                dve.wait_ge(neg_ready, t.count(2, half + 1))
                dve.wait_ge(out_ready, t.count(2, half - 1))
                stt(px_sb[:, blocks, :], neg_sb[:, blocks, :], nal_sb[:], x1_sb[t.slot][:, blocks, :],
                    ALU.mult, ALU.add).then_inc(px_ready, 1)

            def both_parts(t, half):
                blocks = slice(HT * half, HT * (half + 1))
                dve.wait_ge(h2_ready, t.count(2, half + 1))
                nc.vector.tensor_copy(hi_sb[t.slot][:, blocks, :], h2_sb[:, blocks, :]).then_inc(hi_ready, 1)
                dve.wait_ge(hi_ready, t.count(2, half + 1))
                tt(lo_sb[t.slot][:, blocks, :], h2_sb[:, blocks, :], hi_sb[t.slot][:, blocks, :],
                   ALU.subtract).then_inc(lo_ready, 1)

            def finish_last(t, half):
                blocks = slice(HT * half, HT * (half + 1))
                dve.wait_ge(px_ready, t.count(2, half + 1))
                dve.wait_ge(pos_ready, t.count(2, half + 1))
                if half == 0:
                    dve.wait_ge(out_stored[t.slot], 16 * t.use + START)
                tt(out_sb[t.slot][:, blocks, :], px_sb[:, blocks, :], pos_sb[:, blocks, :], ALU.add).then_inc(out_ready, 1)

            def step(k, j):
                front(Batch(k, j + 2))
                add_attention(Batch(k, j + 1))
                middle(Batch(k, j + 1))
                row_exponents(Batch(k, j + 2))
                e_parts(Batch(k, j + 2))
                column_exponents(Batch(k, j + 2))
                add_negative(Batch(k, j), 0)
                column_weights(Batch(k, j + 2))
                g_parts(Batch(k, j + 2))
                add_negative(Batch(k, j), 1)

            start_counts(dve, "dve")
            nc.vector.memset(zero_sb[:], 0.0).then_inc(zero_ready, 1)
            front(Batch(0, 0))
            set_up()
            dve.wait_ge(wa_ready, 1)
            dve.wait_ge(const_in, CONSTS)
            row_exponents(Batch(0, 0))
            column_exponents(Batch(0, 0))
            e_parts(Batch(0, 0))
            column_weights(Batch(0, 0))
            set_up_bias()
            g_parts(Batch(0, 0))
            front(Batch(0, 1))
            add_attention(Batch(0, 0))
            middle(Batch(0, 0))
            row_exponents(Batch(0, 1))
            e_parts(Batch(0, 1))
            column_exponents(Batch(0, 1))
            column_weights(Batch(0, 1))
            g_parts(Batch(0, 1))
            looped(dve, step)
            add_attention(Batch(0, 7))
            middle(Batch(0, 7))
            both_parts(Batch(0, 7), 0)
            add_negative(Batch(0, 6), 0)
            both_parts(Batch(0, 7), 1)
            add_negative(Batch(0, 6), 1)
            add_negative(Batch(0, 7), 0)
            finish_last(Batch(0, 7), 0)
            add_negative(Batch(0, 7), 1)
            finish_last(Batch(0, 7), 1)

        @block.scalar
        def _(act):
            def spread(t):
                act.wait_ge(front_step, t.count(FRONT, 3))
                act.wait_ge(v1_ready, t.count(1))
                nc.scalar.activation(vp_sb[:, 0], df_sb[:, 0], ACT.Square, scale=0.5).then_inc(spread_ready, 1)
                nc.scalar.activation(vp_sb[:, 1], sm_sb[:, 0, :, 1], ACT.Copy, scale=1.0 / F, bias=EPS).then_inc(spread_ready, 1)

            def relu_centred(t):
                act.wait_ge(x_in[t.slot], 16 * t.use + 16)
                act.wait_ge(nm1_ready, t.count(1, 1))
                act.wait_ge(hs_done, t.count(1, 1 - SLOTS))
                for u in range(T):
                    ins = nc.scalar.activation(r1_sb[t.slot][:, u, :], x_sb[t.slot][:, u, :], ACT.Relu,
                                               bias=nm1_sb[t.slot][:, u:u + 1])
                ins.then_inc(r1_ready, 1)

            def row_exponentials(t):
                act.wait_ge(si_ready, t.count(1, 1))
                nc.scalar.activation(e3_sb[t.slot][:, :, 0], s_sb[:, 0, :], ACT.Exp).then_inc(ei_ready, 1)

            def column_exponentials(t):
                act.wait_ge(sj_ready, t.count(1, 1))
                nc.scalar.activation(ej_sb[t.slot][:], s_sb[:, 1, :], ACT.Exp).then_inc(ej_ready, 1)

            def normalise(t, half):
                act.wait_ge(nb2_ready, t.count(1, 1))
                act.wait_ge(lo_ready, t.count(2, 0))
                for u in range(HT * half, HT * (half + 1)):
                    ins = nc.scalar.activation(h2_sb[:, u, :], x1_sb[t.slot][:, u, :], ACT.Relu,
                                               scale=rs2_sb[t.slot][:, u:u + 1], bias=nb2_sb[t.slot][:, u:u + 1])
                ins.then_inc(h2_ready, 1)

            def upper_part(t, half):
                blocks = slice(HT * half, HT * (half + 1))
                act.wait_ge(h2_ready, t.count(2, half + 1))
                nc.scalar.activation(hi_sb[t.slot][:, blocks, :], h2_sb[:, blocks, :], ACT.Copy).then_inc(hi_ready, 1)

            def copy_product(t, h):
                act.wait_ge(y_done, t.count(2, h - 1))
                act.wait_ge(gt_done, t.count(2, h + 1))
                nc.scalar.activation(gt_sb[:, 512 * h:512 * (h + 1)], GT[:, h, :], ACT.Copy,
                                     scale=1.0 / H_SCALE).then_inc(gt_ready, 1)

            y = Y[:].rearrange("p h (u f) -> p (h u) f", f=F)

            def positive(t, half):
                blocks = slice(HT * half, HT * (half + 1))
                act.wait_ge(y_done, t.count(2, half + 1))
                act.wait_ge(out_ready, t.count(2, half - 1))
                nc.scalar.activation(pos_sb[:, blocks, :], y[:, blocks, :], ACT.Relu).then_inc(pos_ready, 1)

            def negative(t, half):
                blocks = slice(HT * half, HT * (half + 1))
                act.wait_ge(y_done, t.count(2, half + 1))
                act.wait_ge(px_ready, t.count(2, half - 1))
                nc.scalar.activation(neg_sb[:, blocks, :], y[:, blocks, :], ACT.Relu, scale=-1.0).then_inc(neg_ready, 1)

            def copy_sum(t):
                act.wait_ge(hs_done, t.count(1, 1))
                act.wait_ge(turned, t.count(1))
                nc.scalar.activation(hr_sb[:], HS[:, 0:F], ACT.Copy).then_inc(hr_ready, 1)

            def spread_sum(t):
                act.wait_ge(turned, t.count(1, 1))
                nc.scalar.activation(hsb_sb[:], S[:, F:2 * F], ACT.Copy).then_inc(hsb_ready, 1)

            def keep_sum(t):
                act.wait_ge(s_done, t.count(1, 1))
                act.wait_ge(x1_ready, t.count(1))
                nc.scalar.activation(ssb_sb[:], S[:, 0:F], ACT.Copy).then_inc(ssb_ready, 1)

            def store(t):
                act.wait_ge(out_ready, t.count(2, 2))
                act.dma_start(out_d[t.index], out_sb[t.slot][:].rearrange("p t f -> p (t f)")).then_inc(out_stored[t.slot], 16)

            def store_half(t, half):
                act.wait_ge(out_ready, t.count(2, half + 1))
                blocks = slice(HT * half, HT * (half + 1))
                act.dma_start(out_d[t.index, :, HT * F * half:HT * F * (half + 1)],
                              out_sb[t.slot][:, blocks, :].rearrange("p t f -> p (t f)")).then_inc(out_stored[t.slot], 16)

            def step(k, j):
                spread(Batch(k, j + 2))
                relu_centred(Batch(k, j + 2))
                copy_product(Batch(k, j), 0)
                negative(Batch(k, j), 0)
                positive(Batch(k, j), 0)
                row_exponentials(Batch(k, j + 2))
                normalise(Batch(k, j + 1), 0)
                copy_product(Batch(k, j), 1)
                upper_part(Batch(k, j + 1), 0)
                column_exponentials(Batch(k, j + 2))
                normalise(Batch(k, j + 1), 1)
                negative(Batch(k, j), 1)
                copy_sum(Batch(k, j + 2))
                positive(Batch(k, j), 1)
                upper_part(Batch(k, j + 1), 1)
                spread_sum(Batch(k, j + 2))
                keep_sum(Batch(k, j + 2))
                store(Batch(k, j))

            act.dma_start(w0t_sb[:], w0t).then_inc(proj_in, 16)
            act.dma_start(a_sb[:], a).then_inc(proj_in, 16)
            act.dma_start(ba_sb[:], bias_a.rearrange("(p t) -> p t", t=T)).then_inc(const_in, 16)
            act.dma_start(al_sb[:], alpha.unsqueeze(0).broadcast_to((P, 1))).then_inc(late_in, 16)
            act.wait_ge(zero_ready, 1)
            nc.scalar.activation(warm_sb[:], zero_sb[:], ACT.Exp).then_inc(warmed, 1)
            start_counts(act, "act")
            relu_centred(Batch(0, 0))
            spread(Batch(0, 0))
            row_exponentials(Batch(0, 0))
            column_exponentials(Batch(0, 0))
            copy_sum(Batch(0, 0))
            spread_sum(Batch(0, 0))
            keep_sum(Batch(0, 0))
            spread(Batch(0, 1))
            relu_centred(Batch(0, 1))
            row_exponentials(Batch(0, 1))
            normalise(Batch(0, 0), 0)
            column_exponentials(Batch(0, 1))
            copy_sum(Batch(0, 1))
            upper_part(Batch(0, 0), 0)
            spread_sum(Batch(0, 1))
            normalise(Batch(0, 0), 1)
            upper_part(Batch(0, 0), 1)
            keep_sum(Batch(0, 1))
            looped(act, step)
            copy_product(Batch(0, 6), 0)
            normalise(Batch(0, 7), 0)
            copy_product(Batch(0, 6), 1)
            negative(Batch(0, 6), 0)
            normalise(Batch(0, 7), 1)
            positive(Batch(0, 6), 0)
            negative(Batch(0, 6), 1)
            positive(Batch(0, 6), 1)
            copy_product(Batch(0, 7), 0)
            store(Batch(0, 6))
            negative(Batch(0, 7), 0)
            positive(Batch(0, 7), 0)
            copy_product(Batch(0, 7), 1)
            negative(Batch(0, 7), 1)
            store_half(Batch(0, 7), 0)
            positive(Batch(0, 7), 1)
            store_half(Batch(0, 7), 1)
            for s in range(SLOTS):
                stores = len(range(s, B, SLOTS)) + (s == (B - 1) % SLOTS)
                act.wait_ge(out_stored[s], 16 * stores + START)

        @block.tensor
        def _(pe):
            mm = nc.tensor.matmul

            def set_up():
                pe.wait_ge(proj_in, PROJ)
                for i in range(2):
                    pe.wait_ge(ab_ready, i + 1)
                    ins = mm(S[:, F * i:F * (i + 1)], ab_sb[:, i, :], w0t_sb[:], start=True, stop=True)
                ins.then_inc(wa_done, 1)

            def times_adj(bank, parts, t, done, chunks):
                for u in range(T):
                    if chunks and u % UC == 0:
                        pe.wait_ge(adj_in[t.slot][u // UC], 16 * t.use + 16)
                    for c in range(T):
                        ins = mm(bank[:, 4 * u:4 * u + PARTS], adj_hi[t.slot][:, u, c, :], parts[t.slot][:, c, :],
                                 start=(c == 0), stop=(c == T - 1))
                ins.then_inc(done, 1)

            def row_sums(t):
                pe.wait_ge(e_ready, t.count(1, 1))
                pe.wait_ge(r_read, t.count(1))
                times_adj(R, e3_hi, t, r_done, True)

            def column_sums(t):
                pe.wait_ge(w_ready, t.count(1, 1))
                pe.wait_ge(hr_ready, t.count(1))
                for u in range(T):
                    q = 32 * (u % 4)
                    ins = mm(HS[q:q + 32, 0:F], w_sb[t.slot][:, u:u + 1].broadcast_to((P, 32)), r1_sb[t.slot][:, u, :],
                             start=(u < 4), stop=(u >= T - 4))
                ins.then_inc(hs_done, 1)

            def turn_sum(t):
                pe.wait_ge(hr_ready, t.count(1, 1))
                pe.wait_ge(ssb_ready, t.count(1))
                mm(S[:, F:2 * F], hr_sb[:], quarter_sb[:], start=True, stop=True).then_inc(turned, 1)

            def spread_projection(t):
                pe.wait_ge(hsb_ready, t.count(1, 1))
                mm(S[:, 0:F], hsb_sb[:], w0_sb[:], start=True, stop=True).then_inc(s_done, 1)

            def weighted(t):
                pe.wait_ge(g_ready, t.count(1, 1))
                pe.wait_ge(q_read, t.count(1))
                times_adj(Q, g3_hi, t, q_done, False)

            def product(t, h, blocks):
                if 0 in blocks:
                    pe.wait_ge(gt_ready, t.count(2, h - 1))
                for c in blocks:
                    if c % HT == 0 or c == blocks[0]:
                        pe.wait_ge(lo_ready, t.count(2, c // HT + 1))
                    for part in (hi_sb, lo_sb):
                        ins = mm(GT[:, h, :], part[t.slot][:, c, :], adj_hi[t.slot][:, HT * h:HT * (h + 1), c, :],
                                 start=(c == 0 and part is hi_sb), stop=(c == T - 1 and part is lo_sb))
                if T - 1 in blocks:
                    ins.then_inc(gt_done, 1)

            def project(t, h):
                pe.wait_ge(pos_ready, t.count(2, h - 1))
                pe.wait_ge(neg_ready, t.count(2, h - 1))
                mm(Y[:, h, :], ones_sb[:], b1p_sb[:].rearrange("p u f -> p (u f)"), start=True, stop=False)
                pe.wait_ge(gt_ready, t.count(2, h + 1))
                for u in range(HT):
                    at = HT * h + u
                    ins = mm(Y[:, h, F * u:F * (u + 1)], gt_sb[:, P * at:P * (at + 1)], w1t_sb[:],
                             start=False, stop=(u == HT - 1))
                ins.then_inc(y_done, 1)

            def step(k, j):
                product(Batch(k, j), 0, range(2, 8))
                product(Batch(k, j), 1, range(0, 2))
                project(Batch(k, j), 0)
                product(Batch(k, j), 1, range(2, 8))
                row_sums(Batch(k, j + 2))
                project(Batch(k, j), 1)
                column_sums(Batch(k, j + 2))
                turn_sum(Batch(k, j + 2))
                weighted(Batch(k, j + 2))
                spread_projection(Batch(k, j + 2))
                product(Batch(k, j + 1), 0, range(0, 2))

            start_counts(pe, "pe")
            set_up()
            column_sums(Batch(0, 0))
            row_sums(Batch(0, 0))
            pe.wait_ge(weights_in, WEIGHTS)
            turn_sum(Batch(0, 0))
            spread_projection(Batch(0, 0))
            weighted(Batch(0, 0))
            row_sums(Batch(0, 1))
            column_sums(Batch(0, 1))
            turn_sum(Batch(0, 1))
            weighted(Batch(0, 1))
            spread_projection(Batch(0, 1))
            product(Batch(0, 0), 0, range(0, 2))
            looped(pe, step)
            product(Batch(0, 6), 0, range(2, 8))
            product(Batch(0, 6), 1, range(0, 2))
            project(Batch(0, 6), 0)
            product(Batch(0, 6), 1, range(2, 8))
            project(Batch(0, 6), 1)
            product(Batch(0, 7), 0, range(T))
            product(Batch(0, 7), 1, range(0, 4))
            project(Batch(0, 7), 0)
            product(Batch(0, 7), 1, range(4, 8))
            project(Batch(0, 7), 1)


def kernel(x, adj, L0_gnn_W, L0_gnn_a, L0_gnn_bias_a, L0_gnn_bias_W, L1_gnn_W, L1_gnn_bias, L1_gnn_prelu_a):
    import numpy as np
    import concourse.bacc as bacc
    from concourse.bass_utils import run_bass_kernel_spmd

    B, N, F = x.shape
    T = N // P
    arrays = {
        "x": np.asarray(x),
        "adj": np.asarray(adj).reshape(B, P, T, P, T).transpose(0, 3, 2, 4, 1),
        "w0": np.asarray(L0_gnn_W),
        "w0t": np.asarray(L0_gnn_W).T,
        "a": np.asarray(L0_gnn_a).reshape(2, F).T,
        "bias_a": np.asarray(L0_gnn_bias_a),
        "bias_w": np.asarray(L0_gnn_bias_W),
        "w1t": np.asarray(L1_gnn_W).T,
        "bias1": np.asarray(L1_gnn_bias),
        "alpha": np.asarray(L1_gnn_prelu_a),
    }
    arrays = {name: np.ascontiguousarray(v) for name, v in arrays.items()}
    nc = bacc.Bacc("TRN2", target_bir_lowering=False, num_devices=1)
    args = [nc.dram_tensor(name, v.shape, mybir.dt.from_np(v.dtype), kind="ExternalInput").ap() for name, v in arrays.items()]
    args.append(nc.dram_tensor("out", (B, N, F), F32, kind="ExternalOutput").ap())
    build(nc, *args)
    result = run_bass_kernel_spmd(nc, [arrays], core_ids=[0])
    return result.results[0]["out"]
```
